# Optimizing a Trainium2 kernel written in Bass

```python
import numpy as np
import jax
import jax.numpy as jnp

def _softmax(x, axis=-1):
    return jax.nn.softmax(x, axis=axis)

def _gelu(x):
    return jax.nn.gelu(x, approximate=True)

def _silu(x):
    return jax.nn.silu(x)

def _sigmoid(x):
    return jax.nn.sigmoid(x)

def _layernorm(x, axis=-1, eps=1e-05):
    m = jnp.mean(x, axis=axis, keepdims=True)
    v = jnp.var(x, axis=axis, keepdims=True)
    return (x - m) / jnp.sqrt(v + eps)

def _scatter_add(tgt, idx, src, axis=0):
    return tgt.at[idx].add(src)

def _segment_sum(src, seg, n):
    return jax.ops.segment_sum(src, seg, n)
kernel_name = 'mk_audio_tower_d1_tok_aud1d256_r4_6942f4'

def setup_inputs(seed: int=0):
    np.random.seed(seed)
    _w = jnp.asarray

    def _rec_inputs():
        import jax
        import jax.numpy as jnp
        _rk = jax.random.key(seed)
        x = 0.000296351 + 0.99907 * jax.random.normal(jax.random.fold_in(_rk, 1), (32, 4096), jnp.float32)
        return x
    x = _rec_inputs()

    def _L0_tok_setup():
        import jax, jax.numpy as jnp
        import numpy as np
        B, L = (64, 4096)
        INTERP_FACTOR = 0.25
        WINDOW, STEP = (64, 64)
        ALPHA, BETA, TEMP = (0.12, 0.9, 1.0)
        A = -0.75

        def _cubic_w(t):
            at = jnp.abs(t)
            w_near = ((A + 2.0) * at - (A + 3.0)) * at * at + 1.0
            w_far = ((A * at - 5.0 * A) * at + 8.0 * A) * at - 4.0 * A
            return jnp.where(at <= 1.0, w_near, jnp.where(at < 2.0, w_far, 0.0))

        def cubic_interpolate_1d(signal, interp_factor):
            b, n = signal.shape
            num_points = int((n - 1) / interp_factor) + 1
            x = jnp.linspace(0.0, 1.0, num_points) * (n - 1)
            i0 = jnp.floor(x).astype(jnp.int32)
            frac = x - i0.astype(x.dtype)
            offs = jnp.arange(-1, 3)
            idx = jnp.clip(i0[:, None] + offs[None, :], 0, n - 1)
            w = _cubic_w(frac[:, None] - offs[None, :].astype(x.dtype))
            taps = signal[:, idx]
            return jnp.einsum('bpk,pk->bp', taps, w)

        def _apply_kernels(x):
            poly = (x + 1.3) ** 2
            gauss = jnp.exp(-0.5 * ((x - 0.7) / 1.0) ** 2)
            return 0.5 * poly + 0.5 * gauss

        def soft_minimum(a, b, temperature):
            b = jnp.broadcast_to(b, a.shape)
            stacked = jnp.stack([-a * temperature, -b * temperature], axis=0)
            return -jax.nn.logsumexp(stacked, axis=0) / temperature

        def _forward(signal):
            interp = cubic_interpolate_1d(signal, INTERP_FACTOR)
            n = interp.shape[1]
            n_windows = (n - WINDOW) // STEP + 1
            starts = jnp.arange(n_windows) * STEP
            idx = starts[:, None] + jnp.arange(WINDOW)[None, :]
            windows = interp[:, idx]
            kw = _apply_kernels(windows)
            M = jnp.abs(jnp.fft.fft(kw, axis=-1))
            Mmax = jnp.max(M, axis=-1, keepdims=True)
            thr = ALPHA * Mmax
            mask = jax.nn.sigmoid((M - thr) * TEMP)
            Mt = M * mask
            return soft_minimum(Mt, BETA * Mmax, TEMP)
        key = jax.random.key(seed)
        return {'signal': jax.random.normal(key, (B, L), dtype=jnp.float32)}
    _L0_tok_all = _L0_tok_setup()
    _L0_tok_in = {k: v for k, v in _L0_tok_all.items() if k in ()}
    del _L0_tok_all

    def _L0_attn_setup():
        import jax, jax.numpy as jnp
        import numpy as np
        key = jax.random.key(seed)
        k1, k2 = jax.random.split(key)
        B, N, F = (4, 1024, 64)
        nodes = jax.random.normal(k1, (B, N, F), dtype=jnp.float32)
        limit = np.sqrt(6.0 / (F + F)).astype(np.float32)
        W = jax.random.uniform(k2, (F, F), dtype=jnp.float32, minval=-limit, maxval=limit)
        return {'nodes': nodes, 'W': W}
    _L0_attn_all = _L0_attn_setup()
    _L0_attn_in = {k: v for k, v in _L0_attn_all.items() if k in ('W',)}
    del _L0_attn_all

    def _L0_ffn_setup():
        import jax, jax.numpy as jnp
        import numpy as np
        DIM = 64
        HEADS = 8
        NUM_KEYS = 64
        NUM_KV = NUM_KEYS ** 2
        PK_TOPK = 16
        FINAL_TOPK = 16
        DIM_KEY = DIM // 2
        P = 2

        def _pk(x, Wq_pk, pk_keys):
            b, n, _ = x.shape
            q = (x @ Wq_pk).reshape(b, n, P, HEADS, DIM_KEY).transpose(2, 0, 1, 3, 4)
            sim = jnp.einsum('pbnhd,pkhd->pbnhk', q, pk_keys)
            scores, idx = jax.lax.top_k(sim, PK_TOPK)
            idx0 = idx[0]
            idx1 = idx[1] * NUM_KEYS
            index = (idx0[..., :, None] + idx1[..., None, :]).reshape(b, n, HEADS, PK_TOPK * PK_TOPK)
            score = (scores[0][..., :, None] + scores[1][..., None, :]).reshape(b, n, HEADS, PK_TOPK * PK_TOPK)
            final_scores, pk_idx = jax.lax.top_k(score, FINAL_TOPK)
            final_indices = jnp.take_along_axis(index, pk_idx, axis=-1)
            final_scores = jax.nn.softmax(final_scores, axis=-1)
            return (final_scores, final_indices)
        key = jax.random.key(seed)
        ks = jax.random.split(key, 7)
        b, n = (2, 256)
        std = 0.02
        x = jax.random.normal(ks[0], (b, n, DIM), dtype=jnp.float32)
        Wq_pk = jax.random.normal(ks[1], (DIM, P * HEADS * DIM_KEY), dtype=jnp.float32) * std
        pk_keys = jax.random.normal(ks[2], (P, NUM_KEYS, HEADS, DIM_KEY), dtype=jnp.float32) * std
        Wq = jax.random.normal(ks[3], (DIM, HEADS * DIM), dtype=jnp.float32) * std
        keys_table = jax.random.normal(ks[4], (NUM_KV * HEADS, DIM), dtype=jnp.float32) * std
        values_table = jax.random.normal(ks[5], (NUM_KV * HEADS, DIM), dtype=jnp.float32) * std
        Wo = jax.random.normal(ks[6], (DIM * HEADS, DIM), dtype=jnp.float32) * std
        return {'x': x, 'Wq_pk': Wq_pk, 'pk_keys': pk_keys, 'Wq': Wq, 'keys_table': keys_table, 'values_table': values_table, 'Wo': Wo}
    _L0_ffn_all = _L0_ffn_setup()
    _L0_ffn_in = {k: v for k, v in _L0_ffn_all.items() if k in ('Wq_pk', 'pk_keys', 'Wq', 'keys_table', 'values_table', 'Wo')}
    del _L0_ffn_all
    return {'x': x, 'L0_attn_W': _L0_attn_in['W'], 'L0_ffn_Wq_pk': _L0_ffn_in['Wq_pk'], 'L0_ffn_pk_keys': _L0_ffn_in['pk_keys'], 'L0_ffn_Wq': _L0_ffn_in['Wq'], 'L0_ffn_keys_table': _L0_ffn_in['keys_table'], 'L0_ffn_values_table': _L0_ffn_in['values_table'], 'L0_ffn_Wo': _L0_ffn_in['Wo']}

def reference(x, L0_attn_W, L0_ffn_Wq_pk, L0_ffn_pk_keys, L0_ffn_Wq, L0_ffn_keys_table, L0_ffn_values_table, L0_ffn_Wo):
    import jax
    import jax.numpy as jnp

    def _L0_tok_ref(signal):
        import jax, jax.numpy as jnp
        import numpy as np
        B, L = (64, 4096)
        INTERP_FACTOR = 0.25
        WINDOW, STEP = (64, 64)
        ALPHA, BETA, TEMP = (0.12, 0.9, 1.0)
        A = -0.75

        def _cubic_w(t):
            at = jnp.abs(t)
            w_near = ((A + 2.0) * at - (A + 3.0)) * at * at + 1.0
            w_far = ((A * at - 5.0 * A) * at + 8.0 * A) * at - 4.0 * A
            return jnp.where(at <= 1.0, w_near, jnp.where(at < 2.0, w_far, 0.0))

        def cubic_interpolate_1d(signal, interp_factor):
            b, n = signal.shape
            num_points = int((n - 1) / interp_factor) + 1
            x = jnp.linspace(0.0, 1.0, num_points) * (n - 1)
            i0 = jnp.floor(x).astype(jnp.int32)
            frac = x - i0.astype(x.dtype)
            offs = jnp.arange(-1, 3)
            idx = jnp.clip(i0[:, None] + offs[None, :], 0, n - 1)
            w = _cubic_w(frac[:, None] - offs[None, :].astype(x.dtype))
            taps = signal[:, idx]
            return jnp.einsum('bpk,pk->bp', taps, w)

        def _apply_kernels(x):
            poly = (x + 1.3) ** 2
            gauss = jnp.exp(-0.5 * ((x - 0.7) / 1.0) ** 2)
            return 0.5 * poly + 0.5 * gauss

        def soft_minimum(a, b, temperature):
            b = jnp.broadcast_to(b, a.shape)
            stacked = jnp.stack([-a * temperature, -b * temperature], axis=0)
            return -jax.nn.logsumexp(stacked, axis=0) / temperature

        def _forward(signal):
            interp = cubic_interpolate_1d(signal, INTERP_FACTOR)
            n = interp.shape[1]
            n_windows = (n - WINDOW) // STEP + 1
            starts = jnp.arange(n_windows) * STEP
            idx = starts[:, None] + jnp.arange(WINDOW)[None, :]
            windows = interp[:, idx]
            kw = _apply_kernels(windows)
            M = jnp.abs(jnp.fft.fft(kw, axis=-1))
            Mmax = jnp.max(M, axis=-1, keepdims=True)
            thr = ALPHA * Mmax
            mask = jax.nn.sigmoid((M - thr) * TEMP)
            Mt = M * mask
            return soft_minimum(Mt, BETA * Mmax, TEMP)
        return _forward(signal)

    def _L0_attn_ref(nodes, W):
        import jax, jax.numpy as jnp
        import numpy as np
        F = nodes.shape[-1]
        norm_const = 1.0 / jnp.sqrt(jnp.asarray(F, dtype=nodes.dtype))
        x = jnp.einsum('bnf,fg->bng', nodes, W)
        prods = jnp.einsum('bnf,bmf->bnm', x, nodes)
        att_scores = jax.nn.softmax(prods * norm_const, axis=-1)
        messgs = jnp.einsum('bnm,bmf->bnf', att_scores, nodes)
        return messgs

    def _L0_ffn_ref(x, Wq_pk, pk_keys, Wq, keys_table, values_table, Wo):
        import jax, jax.numpy as jnp
        import numpy as np
        DIM = 64
        HEADS = 8
        NUM_KEYS = 64
        NUM_KV = NUM_KEYS ** 2
        PK_TOPK = 16
        FINAL_TOPK = 16
        DIM_KEY = DIM // 2
        P = 2

        def _pk(x, Wq_pk, pk_keys):
            b, n, _ = x.shape
            q = (x @ Wq_pk).reshape(b, n, P, HEADS, DIM_KEY).transpose(2, 0, 1, 3, 4)
            sim = jnp.einsum('pbnhd,pkhd->pbnhk', q, pk_keys)
            scores, idx = jax.lax.top_k(sim, PK_TOPK)
            idx0 = idx[0]
            idx1 = idx[1] * NUM_KEYS
            index = (idx0[..., :, None] + idx1[..., None, :]).reshape(b, n, HEADS, PK_TOPK * PK_TOPK)
            score = (scores[0][..., :, None] + scores[1][..., None, :]).reshape(b, n, HEADS, PK_TOPK * PK_TOPK)
            final_scores, pk_idx = jax.lax.top_k(score, FINAL_TOPK)
            final_indices = jnp.take_along_axis(index, pk_idx, axis=-1)
            final_scores = jax.nn.softmax(final_scores, axis=-1)
            return (final_scores, final_indices)
        b, n, d = x.shape
        q = (x @ Wq).reshape(b, n, HEADS, DIM) * DIM ** (-0.5)
        kv_scores, indices = _pk(x, Wq_pk, pk_keys)
        offsets = jnp.arange(HEADS, dtype=indices.dtype) * NUM_KV
        ind = indices + offsets[None, None, :, None]
        k = jnp.einsum('bnhk,bnhkd->bnhd', kv_scores, keys_table[ind])
        v = jnp.einsum('bnhk,bnhkd->bnhd', kv_scores, values_table[ind])
        sim = jnp.einsum('bihd,bjhd->bhij', q, k)
        neg = -jnp.finfo(sim.dtype).max
        causal = jnp.tril(jnp.ones((n, n), dtype=bool))
        sim = jnp.where(causal, sim, neg)
        attn = jax.nn.softmax(sim, axis=-1)
        out = jnp.einsum('bhij,bjhd->bhid', attn, v)
        out = out.transpose(0, 2, 1, 3).reshape(b, n, HEADS * DIM)
        return out @ Wo
    h = _L0_tok_ref(x)
    h = h + _L0_attn_ref(_layernorm(h, axis=-1), L0_attn_W)
    h = h + _L0_ffn_ref(_layernorm(h, axis=-1), L0_ffn_Wq_pk, L0_ffn_pk_keys, L0_ffn_Wq, L0_ffn_keys_table, L0_ffn_values_table, L0_ffn_Wo)
    return h

_drawn_inputs = setup_inputs


def setup_inputs(seed=0):
    import zlib

    import numpy as np

    out = dict(_drawn_inputs(seed))
    spreads = {}
    factors = {'L0_attn_W': 28.474,
     'L0_ffn_Wq_pk': 64.0,
     'L0_ffn_pk_keys': 56.77,
     'L0_ffn_Wq': 64.0,
     'L0_ffn_keys_table': 64.0,
     'L0_ffn_values_table': 64.0,
     'L0_ffn_Wo': 64.0}
    for name, (base, spread) in spreads.items():
        noise = np.random.default_rng([zlib.crc32(name.encode()), seed]).standard_normal(out[name].shape)
        drawn = base * np.exp(spread * noise) if base else spread * noise
        out[name] = jnp.asarray(drawn.astype(out[name].dtype))
    for name, factor in factors.items():
        out[name] = (out[name] * factor).astype(out[name].dtype)
    return out
```

```python
from contextlib import ExitStack

import concourse.bass as bass
from concourse import mybir

F32 = mybir.dt.float32
F32R = mybir.dt.float32r
I32 = mybir.dt.int32
ACT = mybir.ActivationFunctionType
ALU = mybir.AluOpType
AX = mybir.AxisListType

B, L = 32, 4096
UP, WIN = 4, 64
NW = 255
NT = 256
D = 64
QUARTERS = 4
PTS = L * UP // QUARTERS
TAPS = 5
CH = 4
HEADS, NK, TOPK = 8, 64, 16
TILES = B * NT // 128
GT = 4
TOK = GT * 128
GROUPS = TILES // GT
ITERS = HEADS * GROUPS
SLICES = NK * NK // 128
PAIRS = SLICES // 2
PIECE = 4
PIECES = SLICES // PIECE
CAND = [(0, 1, 16), (1, 2, 8), (2, 4, 5), (4, 8, 3), (8, 16, 1)]
NC = sum((hi - lo) * n for lo, hi, n in CAND)
EPS = 1e-5
LOW = -3.0e38
SPREAD = 120.0
EXP_SHIFT = -40.0
HIGH_BITS = -4096


def program(nc, xp, interp_w, dft, ident_d, onehot_d, causal_d, attn_w, wqpk_t, keys_t, table, qo_w, out):
    ctx = ExitStack()
    with ctx:
        def sb(name, shape, dt=F32):
            return ctx.enter_context(nc.sbuf_tensor(name, shape, dt))

        def sem(name):
            return ctx.enter_context(nc.semaphore(name))

        h0_dram = nc.dram_tensor("h0_scratch", (B, NT, D), F32, kind="Internal").ap()
        zt_dram = nc.dram_tensor("zt_scratch", (D, TILES, 128), F32, kind="Internal").ap()

        blk = [sb(f"block{i}", [128, 4096]) for i in range(2)]
        weights_sb = sb("interp_weights", [128, TAPS, PTS])
        blk += [weights_sb[:, i, :] for i in range(TAPS)]
        h_all = sb("h_all", [128, TILES, D])
        ident = sb("ident", [128, 128])
        onehot_f = sb("onehot_f", [128, 8, 128])
        onehot = sb("onehot", [128, 8, 128], F32R)
        causal = sb("causal", [128, 384])
        wattn = sb("wattn", [D, 2, D])
        ctab = sb("ctab", [D, HEADS, 128])
        stats = sb("stats", [128, 8, TILES])

        signal = sb("signal", [128, 1028])
        dft_sb = sb("dft_sb", [128, 128])
        pk_w = sb("pk_w", [32, 2 * HEADS, D])
        pk_k = sb("pk_k", [32, 2 * HEADS, NK])

        interp = blk[0][:, :]
        scr = blk[1][:, :]
        b2, b3, b4, b5, b6 = [blk[i] for i in range(2, 7)]

        tab = blk[0][:, :].rearrange("p (c n) -> p c n", c=SLICES)
        wgt = b2.rearrange("p (b c n) -> p b c n", b=4, c=2)
        esum = b3[:, 0:2048].rearrange("p (b c n) -> p b c n", b=2, c=2)
        rsum = sb("rsum", [128, 4, TOK], F32R)
        z_sel = sb("z_sel", [D, TOK])
        z_att = sb("z_att", [D, TOK])
        qo = sb("qo", [D, 2, D])
        score = b4[:, 0:512].rearrange("p (t s k) -> p t s k", t=GT, s=2)
        score_m = b4[:, 512:1024].rearrange("p (t s k) -> p t s k", t=GT, s=2)
        shifted = b4[:, 1024:1280].rearrange("p (t k) -> p t k", t=GT)
        parts = sb("parts", [128, GT, 2, 2, 2, 2, 32])
        top = sb("top", [128, GT, 2, TOPK])
        cand = sb("cand", [128, GT, NC])
        cand_m = sb("cand_m", [128, GT, NC])
        cand_mm = sb("cand_mm", [128, GT, NC])
        best = sb("best", [128, GT, TOPK])
        small = sb("small", [128, 8, GT])
        wbest = sb("wbest", [128, GT, TOPK])
        wsel = sb("wsel", [128, GT, TOPK])
        rz_new = sb("rz_new", [128, GT])
        rz = sb("rz", [128, GT])
        kv_a = b4[:, 1536:2048]
        kv_t = b4[:, 2048:2560]
        kv_n = b4[:, 2560:3072].rearrange("p (t d) -> p t d", t=GT)
        k_t = b4[0:D, 3072:3584]
        q_t = b4[0:D, 3584:4096]
        simm = b5[:, 0:768].rearrange("p (x n) -> p x n", x=2)
        prob = b5[:, 768:1536].rearrange("p (x n) -> p x n", x=2)
        prob_t = b5[:, 1536:2304].rearrange("p (x n) -> p x n", x=2)
        o_t = b5[0:D, 2304:2816]
        nmax = sb("nmax", [128, 4])
        lsum = sb("lsum", [128, 4])
        rl = sb("rl", [128, 4])
        y_n = sb("y_n", [128, GT, D])
        gate = sb("gate", [128, 2])
        m40 = sb("m40", [128, 4])

        ybank = [ctx.enter_context(nc.psum_tensor(f"ybank{i}", [128, 2, 512], F32)) for i in range(2)]
        acc = [ctx.enter_context(nc.psum_tensor(f"acc{i}", [128, 512], F32)) for i in range(2)]
        misc = [ctx.enter_context(nc.psum_tensor(f"misc{i}", [128, 512], F32)) for i in range(2)]
        bank = [ybank[0][:, 0, :], ybank[0][:, 1, :], ybank[1][:, 0, :], ybank[1][:, 1, :],
                acc[0][:, :], acc[1][:, :], misc[0][:, :], misc[1][:, :]]

        ld_small, ld_sig = sem("ld_small"), sem("ld_sig")
        ld_w = [sem(f"ld_w{c}") for c in range(CH)]
        const_ready = sem("const_ready")
        interp_done, squares_done, kw_done = sem("interp_done"), sem("squares_done"), sem("kw_done")
        kwt_pe, kwt_act = sem("kwt_pe"), sem("kwt_act")
        dft_pe, dft_act = sem("dft_pe"), sem("dft_act")
        a_dve, a_act = sem("a_dve"), sem("a_act")
        h0_stored, h0_loaded = sem("h0_stored"), sem("h0_loaded")
        xs_done, xt_pe, xt_act, xw_pe, xw_dve = (sem(n) for n in ("xs_done", "xt_pe", "xt_act", "xw_pe", "xw_dve"))
        s_pe, smax_done, p_act, pt_pe, pt_act, pt_dve, msg_pe, h1_done = (
            sem(n) for n in ("s_pe", "smax_done", "p_act", "pt_pe", "pt_act", "pt_dve", "msg_pe", "h1_done"))
        zt_pe, zt_act, zt_stored, ctab_pe, ctab_act = (
            sem(n) for n in ("zt_pe", "zt_act", "zt_stored", "ctab_pe", "ctab_act"))
        link_a = sem("link_a")
        z_sel_in, z_att_in, qo_in = sem("z_sel_in"), sem("z_att_in"), sem("qo_in")
        tab_in = [sem(f"tab_in{p}") for p in range(PIECES)]
        scores_pe, score_act, select_step, low_pool = (
            sem(n) for n in ("scores_pe", "score_act", "select_step", "low_pool"))
        quad_pe, quad_act = sem("quad_pe"), sem("quad_act")
        y_done, e_done, w_done, gather_done = sem("y_done"), sem("e_done"), sem("w_done"), sem("gather_done")
        kva_act, kvt_dve, kvn_pe, kvn_dve = sem("kva_act"), sem("kvt_dve"), sem("kvn_pe"), sem("kvn_dve")
        q_pe, q_act, kt_pe, kt_act = sem("q_pe"), sem("q_act"), sem("kt_pe"), sem("kt_act")
        sim_pe, simm_dve, prob_act = sem("sim_pe"), sem("simm_dve"), sem("prob_act")
        probt_pe, probt_act, o_pe, o_act, y_pe, h_dve = (
            sem(n) for n in ("probt_pe", "probt_act", "o_pe", "o_act", "y_pe", "h_dve"))
        rz_link, out_stored = sem("rz_link"), sem("out_stored")
        smax_link, r_link, sim_link, rl_link, rzn_link, rzn_done = (
            sem(n) for n in ("smax_link", "r_link", "sim_link", "rl_link", "rzn_link", "rzn_done"))
        wexp_act, guard_dve = sem("wexp_act"), sem("guard_dve")

        SEL = 13
        QUAD_SLOTS = (11, 13, 14, 15)
        PLACES = []
        for other in range(2):
            PLACES.append((parts[:, :, :, other, 0, 0, :], parts[:, :, :, other, 0, 1, :],
                           score[:, :, 0, :].rearrange("p t (a k) -> p t a k", a=2)))
            PLACES.append((parts[:, :, other, :, 1, 0, :], parts[:, :, other, :, 1, 1, :],
                           shifted.rearrange("p t (a k) -> p t a k", a=2)))
        block = ctx.enter_context(nc.Block())

        def static(it):
            return isinstance(it, int)

        def flags(it):
            if not static(it):
                return True, True, True
            return it + 1 < ITERS, 0 <= it < ITERS, it >= 1

        def pair_of(it, s):
            owner = it if s + 2 < PAIRS else it + 1
            if static(it) and not 0 <= owner < ITERS:
                return None
            return it * PAIRS + s + 2, (s + 2) % PAIRS, owner

        def wait(eng, s, value):
            if static(value) and value <= 0:
                return
            eng.wait_ge(s, value)

        def run_iterations(eng, body):
            for it in (-1, 0, 1):
                body(it)
            with eng.Fori(2, ITERS - 1) as it:
                body(it)
            body(ITERS - 1)
            body(ITERS)

        @block.sync
        def _(sp):
            sp.dma_start(ident[:, :], ident_d).then_inc(ld_small, 16)
            sp.dma_start(dft_sb[:, :], dft).then_inc(ld_small, 16)
            sp.dma_start(onehot_f[:, :, :], onehot_d).then_inc(ld_small, 16)
            sp.dma_start(causal[:, :], causal_d).then_inc(ld_small, 16)
            for i in range(2):
                sp.dma_start(wattn[:, i, :], attn_w).then_inc(ld_small, 16)
            sp.dma_start(pk_w[:, :, :], wqpk_t).then_inc(ld_small, 16)
            sp.dma_start(pk_k[:, :, :], keys_t).then_inc(ld_small, 16)
            sp.wait_ge(a_dve, 9)
            for q in range(QUARTERS):
                sp.dma_start(h0_dram[:, q * 64:(q + 1) * 64, :],
                             interp[32 * q:32 * q + 32, :].rearrange("b (w f) -> b w f", w=64)).then_inc(h0_stored, 16)
            sp.wait_ge(h0_stored, 16 * QUARTERS)
            sp.dma_start(h_all[:, 0:TILES // 2, :],
                         h0_dram[0:B // 2].rearrange("b (nh p) f -> p (b nh) f", p=128)).then_inc(h0_loaded, 16)
            sp.dma_start(h_all[:, TILES // 2:TILES, :],
                         h0_dram[B // 2:B].rearrange("b (nh p) f -> p (b nh) f", p=128)).then_inc(h0_loaded, 16)
            sp.wait_ge(zt_act, 8)
            ztv = zt_dram.rearrange("d (t o) n -> o d t n", o=2)
            zsb = b2.rearrange("p (t n) -> p t n", n=128)
            sp.dma_start(ztv[0], zsb[0:64]).then_inc(zt_stored, 16)
            sp.dma_start(ztv[1], zsb[64:128]).then_inc(zt_stored, 16)
            sp.wait_ge(zt_stored, 32)

            def load_select(j, g):
                wait(sp, scores_pe, j)
                sp.dma_start(z_sel[:, :].rearrange("d (t n) -> d t n", t=GT),
                             zt_dram[:, bass.ds(g * GT, GT), :]).then_inc(z_sel_in, 16)

            def load_attend(j, g, h):
                wait(sp, y_pe, j)
                sp.dma_start(z_att[:, :].rearrange("d (t n) -> d t n", t=GT),
                             zt_dram[:, bass.ds(g * GT, GT), :]).then_inc(z_att_in, 16)
                sp.dma_start(qo[:, :, :], qo_w[bass.ds(h, 1)].rearrange("a d k n -> (a d) k n")).then_inc(qo_in, 16)

            def load_table(h):
                for p in range(PIECES):
                    wait(sp, gather_done, h * GROUPS * PAIRS - PAIRS + 2 * (p + 1))
                    sp.dma_start(tab[:, p * PIECE:(p + 1) * PIECE, :],
                                 table[bass.ds(h, 1), :, p * PIECE:(p + 1) * PIECE, :]
                                 .rearrange("a p c n -> (a p) c n")).then_inc(tab_in[p], 16)

            load_select(0, 0)
            load_table(0)
            load_select(1, 1)
            load_select(2, 2)
            load_attend(0, 0, 0)

            def head_steps(h, first, end):
                with sp.Fori(first, end) as g:
                    load_select(h * GROUPS + g + 2, (g + 2) % GROUPS)
                    load_attend(h * GROUPS + g, g, h)

            head_steps(0, 1, GROUPS)
            load_table(1)
            with sp.Fori(1, HEADS - 1) as h:
                head_steps(h, 0, GROUPS)
                load_table(h + 1)
            head_steps(HEADS - 1, 0, GROUPS - 2)
            for g in (GROUPS - 2, GROUPS - 1):
                load_attend((HEADS - 1) * GROUPS + g, g, HEADS - 1)
            sp.wait_ge(h_dve, ITERS)
            hv = h_all[:, :, :].rearrange("p (b o) f -> p b o f", o=2)
            sp.dma_start(out[:, 0:128, :].rearrange("b p f -> p b f"), hv[:, :, 0, :]).then_inc(out_stored, 16)
            sp.dma_start(out[:, 128:NW, :].rearrange("b p f -> p b f"), hv[0:NW - 128, :, 1, :]).then_inc(out_stored, 16)
            sp.wait_ge(out_stored, 32)

        @block.gpsimd
        def _(pool):
            for s in range(QUARTERS):
                pool.dma_start(signal[32 * s:32 * s + 32, :], xp[:, 1024 * s:1024 * s + 1028]).then_inc(ld_sig, 16)
            for c in range(CH):
                for s in range(QUARTERS):
                    pool.dma_start(weights_sb[32 * s:32 * s + 32, :, 1024 * c:1024 * (c + 1)],
                                   interp_w[s, :, 1024 * c:1024 * (c + 1)].partition_broadcast(32)).then_inc(ld_w[c], 16)

            def body(it):
                if flags(it)[0]:
                    wait(pool, select_step, SEL * (it + 1) + SEL)
                    for high, low, src in PLACES:
                        last = nc.gpsimd.tensor_tensor(low, src, high, ALU.subtract)
                    last.then_inc(low_pool, 1)

            run_iterations(pool, body)

        @block.scalar
        def _(act):
            act.wait_ge(ld_small, 16 * 8)
            nc.scalar.activation(onehot[:, :, :], onehot_f[:, :, :], ACT.Copy).then_inc(const_ready, 1)
            act.wait_ge(ctab_pe, 1)
            for i in range(2):
                nc.scalar.activation(ctab[:, 4 * i:4 * i + 4, :],
                                     ybank[0][0:D, i, :].rearrange("p (h n) -> p h n", h=4), ACT.Copy)\
                  .then_inc(ctab_act, 1)
            act.wait_ge(guard_dve, 1)
            for c in range(CH):
                sl = slice(1024 * c, 1024 * (c + 1))
                act.wait_ge(interp_done, c + 1)
                nc.scalar.activation(scr[:, sl], interp[:, sl], ACT.Square, bias=m40[:, 1:2]).then_inc(squares_done, 1)
                act.wait_ge(squares_done, 3 * c + 1)
                nc.scalar.activation(weights_sb[:, 0, sl], scr[:, sl], ACT.Exp, scale=-0.5).then_inc(squares_done, 1)
                nc.scalar.activation(weights_sb[:, 1, sl], interp[:, sl], ACT.Square, bias=m40[:, 2:3])\
                    .then_inc(squares_done, 1)
            for g in range(8):
                act.wait_ge(kwt_pe, g + 1)
                nc.scalar.activation(b4[:, 512 * g:512 * (g + 1)], bank[g], ACT.Copy).then_inc(kwt_act, 1)
            for g in range(16):
                dst = (b2 if g < 8 else b3)[:, 512 * (g % 8):512 * (g % 8) + 512]
                act.wait_ge(dft_pe, g + 1)
                nc.scalar.activation(dst, bank[g % 8], ACT.Square).then_inc(dft_act, 1)
            act.wait_ge(a_dve, 1)
            nc.scalar.activation(b6, b5, ACT.Sqrt).then_inc(a_act, 1)
            act.wait_ge(a_dve, 3)
            nc.scalar.activation(b3, b2, ACT.Sigmoid).then_inc(a_act, 1)
            act.wait_ge(a_dve, 5)
            nc.scalar.activation(b3, b2, ACT.Abs).then_inc(a_act, 1)
            act.wait_ge(a_act, 3)
            nc.scalar.activation(b5, b3, ACT.Exp, scale=-1.0).then_inc(a_act, 1)
            act.wait_ge(a_act, 4)
            nc.scalar.activation(b4, b5, ACT.Ln, bias=1.0).then_inc(a_act, 1)

            def norm_act(dve_at, act_at):
                act.wait_ge(a_dve, dve_at)
                nc.scalar.activation(b4, b3, ACT.Square).then_inc(a_act, 1)
                act.wait_ge(a_dve, dve_at + 2)
                nc.scalar.activation(stats[:, 2, :], stats[:, 1, :], ACT.Sqrt).then_inc(a_act, 1)

            norm_act(11, 5)
            with act.Fori(0, 8) as a:
                act.wait_ge(xt_pe, a + 1)
                nc.scalar.activation(b4[0:D, 0:1024].rearrange("p (c n) -> p c n", c=2), ybank[0][0:D], ACT.Copy)\
                    .then_inc(xt_act, 1)
                for y in range(2):
                    act.wait_ge(smax_done, 2 * a + y + 1)
                    for t in range(4):
                        last = nc.scalar.activation(
                            b5[:, (4 * y + t) * 256:(4 * y + t) * 256 + NW],
                            ybank[y][:, t // 2, (t % 2) * 256:(t % 2) * 256 + NW],
                            ACT.Exp, bias=stats[:, 5, 4 * y + t:4 * y + t + 1], scale=0.125,
                            accum_out=stats[:, 6, 4 * y + t:4 * y + t + 1])
                    last.then_inc(p_act, 1)
                for i in range(2):
                    act.wait_ge(pt_pe, 4 * a + i + 1)
                    nc.scalar.activation(b2[:, 512 * i:512 * (i + 1)], bank[4 + i], ACT.Copy).then_inc(pt_act, 1)
            norm_act(15, 7)
            for g in range(8):
                act.wait_ge(zt_pe, g + 1)
                nc.scalar.activation(b2[:, 512 * g:512 * (g + 1)], bank[g], ACT.Copy).then_inc(zt_act, 1)

            def slot(it, s):
                select, gather, attend = flags(it)
                pair = pair_of(it, s)
                if pair:
                    n, u, _own = pair
                    wait(act, y_done, n + 1)
                    wait(act, w_done, n - 1)
                    nc.scalar.activation(esum[:, s % 2, :, :], ybank[s % 2][:, :, :], ACT.Exp,
                                         bias=m40[:, 0:1]).then_inc(e_done, 1)
                if s == 0 and select:
                    j = it + 1
                    wait(act, scores_pe, j + 1)
                    wait(act, low_pool, j)
                    nc.scalar.activation(score, misc[0][:, :].rearrange("p (t s k) -> p t s k", t=GT, s=2),
                                         ACT.Copy).then_inc(score_act, 1)
                if s == 3 and attend:
                    j = it - 1
                    wait(act, q_pe, j + 1)
                    nc.scalar.activation(q_t, misc[1][0:D, :], ACT.Copy, scale=0.125).then_inc(q_act, 1)
                if s == 4 and attend:
                    j = it - 1
                    wait(act, kt_pe, j + 1)
                    nc.scalar.activation(k_t, misc[1][0:D, :], ACT.Copy).then_inc(kt_act, 1)
                if s == 8 and gather:
                    wait(act, gather_done, PAIRS * it + PAIRS // 2)
                    wait(act, kvt_dve, it)
                    nc.scalar.activation(kv_a, acc[0][:, :], ACT.Copy).then_inc(kva_act, 1)
                if s in (10, 11) and attend:
                    j, x = it - 1, s - 10
                    wait(act, simm_dve, 4 * j + 2 * x + 2)
                    wait(act, h_dve, j)
                    nc.scalar.activation(prob[:, x, 0:128], simm[:, x, 0:128], ACT.Exp,
                                         bias=nmax[:, 2 * x:2 * x + 1], accum_out=lsum[:, 2 * x:2 * x + 1])
                    nc.scalar.activation(prob[:, x, 128:384], simm[:, x, 128:384], ACT.Exp,
                                         bias=nmax[:, 2 * x + 1:2 * x + 2],
                                         accum_out=lsum[:, 2 * x + 1:2 * x + 2]).then_inc(prob_act, 1)
                if s in (12, 13) and attend:
                    j, x = it - 1, s - 12
                    wait(act, probt_pe, 2 * j + x + 1)
                    nc.scalar.activation(prob_t[:, x, :], misc[x][:, 0:384], ACT.Copy).then_inc(probt_act, 1)
                if s == 14 and attend:
                    j = it - 1
                    wait(act, o_pe, j + 1)
                    nc.scalar.activation(o_t, misc[1][0:D, :], ACT.Copy).then_inc(o_act, 1)
                if s in QUAD_SLOTS and select:
                    j, quad = it + 1, QUAD_SLOTS.index(s)
                    wait(act, quad_pe, 4 * j + quad + 1)
                    if gather:
                        wait(act, y_done, PAIRS * it + 4 * (quad + 1))
                    nc.scalar.activation(rsum[:, quad, :], misc[0][:, :], ACT.Copy).then_inc(quad_act, 1)
                if s == 12 and select:
                    j = it + 1
                    wait(act, select_step, SEL * j + SEL)
                    nc.scalar.activation(wbest[:, :, :], wsel[:, :, :], ACT.Exp, bias=m40[:, 0:1]).then_inc(wexp_act, 1)

            def body(it):
                for s in range(PAIRS):
                    slot(it, s)

            run_iterations(act, body)

        @block.tensor
        def _(pe):
            pe.wait_ge(ld_small, 16 * 8)
            for h in range(HEADS):
                for half in range(2):
                    i = 2 * h + half
                    last = nc.tensor.matmul(ybank[0][0:D, h // 4, (h % 4) * 128 + 64 * half:(h % 4) * 128 + 64 * half + 64],
                                            pk_w[:, i, :], pk_k[:, i, :], start=True, stop=True)
            last.then_inc(ctab_pe, 1)
            pe.wait_ge(ctab_act, 2)
            for g in range(8):
                pe.wait_ge(kw_done, g // 2 + 1)
                for i in range(4):
                    c = (4 * g + i) * 128
                    last = nc.tensor.transpose(bank[g][:, 128 * i:128 * i + 128], b5[:, c:c + 128], ident[:, :])
                last.then_inc(kwt_pe, 1)
            kwt = b4.rearrange("p (w n) -> p w n", n=128)
            for g in range(16):
                pe.wait_ge(kwt_act, max(g // 2 + 1, g + 1 if g < 8 else 8))
                if g >= 8:
                    pe.wait_ge(dft_act, g - 7)
                for i in range(4):
                    w = 8 * (g // 2) + 2 * i + g % 2
                    lo = 64 * (w % 2)
                    last = nc.tensor.matmul(bank[g % 8][:, 128 * i:128 * i + 128], kwt[lo:lo + 64, w // 2, :],
                                            dft_sb[lo:lo + 64, :], start=True, stop=True)
                last.then_inc(dft_pe, 1)
            pe.wait_ge(dft_act, 16)
            xs = b6[:, 0:512].rearrange("p (t f) -> p t f", t=8)
            with pe.Fori(0, 8) as a:
                pe.wait_ge(xs_done, a + 1)
                pe.wait_ge(h1_done, a + 1)
                for t in range(8):
                    last = nc.tensor.transpose(ybank[0][:, t // 4, (t % 4) * 128:(t % 4) * 128 + 128],
                                               b6[:, 64 * t:64 * t + 128], ident[:, :])
                last.then_inc(xt_pe, 1)
                pe.wait_ge(xt_act, a + 1)
                for i in range(2):
                    last = nc.tensor.matmul(ybank[1][:, i, :], wattn[:, :, :].rearrange("p a n -> p (a n)"), b4[0:D, 512 * i:512 * (i + 1)],
                                            start=True, stop=True)
                last.then_inc(xw_pe, 1)
                pe.wait_ge(xw_dve, a + 1)
                for y in range(2):
                    for t in range(4):
                        tile = 4 * y + t
                        last = nc.tensor.matmul(ybank[y][:, t // 2, (t % 2) * 256:(t % 2) * 256 + NW],
                                                b4[0:D, 1024 + 128 * tile:1024 + 128 * tile + 128],
                                                b4[0:D, 256 * (tile // 2):256 * (tile // 2) + NW],
                                                start=True, stop=True)
                    last.then_inc(s_pe, 1)
                for t in range(8):
                    if t % 4 == 0:
                        pe.wait_ge(p_act, 2 * a + t // 4 + 1)
                    for mh in range(2):
                        last = nc.tensor.transpose(
                            bank[4 + t // 2][:, (2 * (t % 2) + mh) * 128:(2 * (t % 2) + mh) * 128 + 128],
                            b5[:, t * 256 + 128 * mh:t * 256 + 128 * mh + 128], ident[:, :])
                    if t % 2:
                        last.then_inc(pt_pe, 1)
                pe.wait_ge(pt_act, 2 * a + 2)
                pe.wait_ge(pt_dve, 2 * a + 2)
                for t in range(8):
                    for mh in range(2):
                        c = (2 * t + mh) * 128
                        last = nc.tensor.matmul(ybank[0][:, 0, 64 * t:64 * t + 64], b2[:, c:c + 128],
                                                xs[:, 2 * (t // 2) + mh, :], start=(mh == 0), stop=(mh == 1))
                last.then_inc(msg_pe, 1)
            pe.wait_ge(a_dve, 18)
            for g in range(8):
                for i in range(4):
                    c = (4 * g + i) * 128
                    last = nc.tensor.transpose(bank[g][:, 128 * i:128 * i + 128], b6[:, c:c + 128], ident[:, :])
                last.then_inc(zt_pe, 1)
            pe.wait_ge(zt_act, 8)

            def slot(it, s):
                select, gather, attend = flags(it)
                if gather:
                    wait(pe, w_done, PAIRS * it + s + 1)
                pair = pair_of(it, s)
                if pair:
                    n, u, own = pair
                    quad = u // 4
                    if u % 4 == 0:
                        wait(pe, quad_act, 4 * own + quad + 1)
                    for c in range(2):
                        last = nc.tensor.matmul(ybank[s % 2][:, c, :], onehot[:, (2 * u + c) % 8, :], rsum[:, quad, :],
                                                start=True, stop=True)
                    last.then_inc(y_done, 1)
                if s == 0 and select:
                    j = it + 1
                    wait(pe, z_sel_in, 16 * (j + 1))
                    wait(pe, quad_act, 4 * j)
                    for t in range(GT):
                        last = nc.tensor.matmul(misc[0][:, 128 * t:128 * t + 128], z_sel[:, 128 * t:128 * t + 128],
                                                ctab[:, bass.ds(j // GROUPS, 1), :].rearrange("p a n -> p (a n)"),
                                                start=True, stop=True)
                    last.then_inc(scores_pe, 1)
                if s == 2 and attend:
                    j = it - 1
                    wait(pe, kvt_dve, j + 1)
                    if select:
                        wait(pe, score_act, it + 2)
                    else:
                        wait(pe, quad_act, 4 * ITERS)
                    for t in range(GT):
                        last = nc.tensor.transpose(misc[0][:, 128 * t:128 * t + 128], kv_t[:, 128 * t:128 * t + 128],
                                                   ident[:, :])
                    last.then_inc(kvn_pe, 1)
                if s == 3 and attend:
                    j = it - 1
                    wait(pe, qo_in, 16 * (j + 1))
                    wait(pe, z_att_in, 16 * (j + 1))
                    wait(pe, h_dve, j)
                    nc.tensor.matmul(misc[1][:, :], qo[:, :, :].rearrange("p a n -> p (a n)"), z_att[:, :],
                                     start=True, stop=True).then_inc(q_pe, 1)
                if s == 4 and attend:
                    j = it - 1
                    wait(pe, kvn_dve, j + 1)
                    wait(pe, q_act, j + 1)
                    for t in range(GT):
                        last = nc.tensor.transpose(misc[1][:, 128 * t:128 * t + 128], kv_n[:, t, :], ident[:, :])
                    last.then_inc(kt_pe, 1)
                if s in (8, 9) and attend:
                    j, x = it - 1, s - 8
                    wait(pe, kt_act, j + 1)
                    c = 256 * x
                    nc.tensor.matmul(misc[x][:, 0:128], q_t[:, c:c + 128], k_t[:, c:c + 128], start=True, stop=True)
                    nc.tensor.matmul(misc[x][:, 128:384], q_t[:, c + 128:c + 256], k_t[:, c:c + 256],
                                     start=True, stop=True).then_inc(sim_pe, 1)
                if s in (12, 13) and attend:
                    j, x = it - 1, s - 12
                    wait(pe, prob_act, 2 * j + x + 1)
                    if x == 0 and select:
                        wait(pe, quad_act, 4 * (it + 1) + 1)
                    for i in range(3):
                        last = nc.tensor.transpose(misc[x][:, 128 * i:128 * i + 128],
                                                   prob[:, x, 128 * i:128 * i + 128], ident[:, :])
                    last.then_inc(probt_pe, 1)
                if s in QUAD_SLOTS and select:
                    j, quad = it + 1, QUAD_SLOTS.index(s)
                    ka, kb = quad // 2, quad % 2
                    if quad == 0:
                        wait(pe, low_pool, j + 1)
                        if attend:
                            wait(pe, simm_dve, 4 * (it - 1) + 2)
                    else:
                        wait(pe, quad_act, 4 * j + quad)
                        if quad == 1 and attend:
                            wait(pe, probt_act, 2 * (it - 1) + 1)
                    for t in range(GT):
                        src = parts[:, t, ka, kb].rearrange("p s c k -> p (s c k)")
                        last = nc.tensor.transpose(misc[0][:, 128 * t:128 * t + 128], src, ident[:, :])
                    last.then_inc(quad_pe, 1)
                if s == 14 and attend:
                    j = it - 1
                    wait(pe, probt_act, 2 * j + 2)
                    for x in range(2):
                        c = 256 * x
                        nc.tensor.matmul(misc[1][0:D, c:c + 256], kv_n[:, 2 * x, D:2 * D], prob_t[:, x, 0:256],
                                         start=True, stop=False)
                        last = nc.tensor.matmul(misc[1][0:D, c + 128:c + 256], kv_n[:, 2 * x + 1, D:2 * D],
                                                prob_t[:, x, 256:384], start=False, stop=True)
                    last.then_inc(o_pe, 1)
                if s == 15 and attend:
                    j = it - 1
                    wait(pe, o_act, j + 1)
                    for t in range(GT):
                        last = nc.tensor.matmul(misc[1][:, 64 * t:64 * t + 64], o_t[:, 128 * t:128 * t + 128],
                                                qo[:, 1, :], start=True, stop=True)
                    last.then_inc(y_pe, 1)
                if gather:
                    if s % 2 == 0:
                        wait(pe, tab_in[s // 2], 16 * (it // GROUPS + 1))
                    if s == 0:
                        wait(pe, kva_act, it)
                    if s == PAIRS // 2:
                        wait(pe, kvt_dve, it)
                    half = s // (PAIRS // 2)
                    for c in range(2):
                        k = 2 * s + c
                        last = nc.tensor.matmul(acc[half][:, :], tab[:, k, :], wgt[:, s % 4, c, :],
                                                start=(k % (SLICES // 2) == 0), stop=(k % (SLICES // 2) == SLICES // 2 - 1))
                    last.then_inc(gather_done, 1)

            def body(it):
                for s in range(PAIRS):
                    slot(it, s)

            run_iterations(pe, body)

        @block.vector
        def _(dve):
            steps = [0]

            def link(ins):
                steps[0] += 1
                ins.then_inc(link_a, 1)
                dve.wait_ge(link_a, steps[0])

            nc.vector.memset(gate[:, :], 0.0)
            nc.vector.memset(m40[:, 0:1], EXP_SHIFT)
            nc.vector.memset(m40[:, 1:2], -0.7)
            nc.vector.memset(m40[:, 2:3], 1.3).then_inc(guard_dve, 1)
            dve.wait_ge(ld_sig, 16 * QUARTERS)

            def kernels(c):
                sl = slice(1024 * c, 1024 * (c + 1))
                dve.wait_ge(squares_done, 3 * c + 3)
                link(nc.vector.tensor_tensor(weights_sb[:, 2, sl], weights_sb[:, 0, sl], weights_sb[:, 1, sl], ALU.add))
                nc.vector.tensor_scalar(b5[:, sl], weights_sb[:, 2, sl], 0.5, None, ALU.mult).then_inc(kw_done, 1)

            for c in range(CH):
                dve.wait_ge(ld_w[c], 16 * QUARTERS)

                def v(ap):
                    return ap[:, 1024 * c:1024 * (c + 1)].rearrange("p (s f) -> p s f", f=UP)

                def x(k):
                    return signal[:, 256 * c + k:256 * c + k + 256].unsqueeze(2).broadcast_to([128, 256, UP])

                link(nc.vector.tensor_tensor(v(interp), v(blk[2]), x(0), ALU.mult))
                for k in range(1, TAPS):
                    link(nc.vector.tensor_tensor(v(scr), v(blk[2 + k]), x(k), ALU.mult))
                    last = nc.vector.tensor_tensor(v(interp), v(interp), v(scr), ALU.add)
                    if k < TAPS - 1:
                        link(last)
                last.then_inc(interp_done, 1)
                if c >= 1:
                    kernels(c - 1)
            kernels(CH - 1)

            t3 = lambda ap: ap.rearrange("p (t f) -> p t f", f=D)
            st = lambda i: stats[:, i, :]
            wide = lambda i: stats[:, i, :].unsqueeze(2).broadcast_to([128, TILES, D])

            def step(ins):
                ins.then_inc(a_dve, 1)

            for g in range(2):
                dve.wait_ge(dft_act, 8 * (g + 1))
                sq = (b2, b3)[g].rearrange("p (c o i r f) -> p c o i r f", c=4, o=2, i=4, r=2)
                for o in range(2):
                    last = nc.vector.tensor_tensor(
                        b5[:, 2048 * g:2048 * (g + 1)].rearrange("p (c i o f) -> p c o i f", c=4, i=4, o=2)[:, :, o],
                        sq[:, :, o, :, 0, :], sq[:, :, o, :, 1, :], ALU.add)
            step(last)
            dve.wait_ge(a_act, 1)
            step(nc.vector.tensor_reduce(st(0), t3(b6), AX.X, ALU.max))
            dve.wait_ge(a_dve, 2)
            step(nc.vector.scalar_tensor_tensor(t3(b2), wide(0), -0.12, t3(b6), ALU.mult, ALU.add))
            dve.wait_ge(a_act, 2)
            step(nc.vector.tensor_tensor(b4, b6, b3, ALU.mult))
            dve.wait_ge(a_dve, 4)
            step(nc.vector.scalar_tensor_tensor(t3(b2), wide(0), -0.9, t3(b4), ALU.mult, ALU.add))
            dve.wait_ge(a_dve, 5)
            step(nc.vector.tensor_scalar(b6, b2, 0.0, None, ALU.min))
            dve.wait_ge(a_dve, 6)
            step(nc.vector.scalar_tensor_tensor(t3(b6), wide(0), 0.9, t3(b6), ALU.mult, ALU.add))
            dve.wait_ge(a_act, 5)
            dve.wait_ge(a_dve, 7)
            step(nc.vector.tensor_tensor(interp, b6, b4, ALU.subtract))
            dve.wait_ge(a_dve, 8)
            step(nc.vector.memset(b5[:, :], 0.0))
            dve.wait_ge(h0_loaded, 32)

            def norm_dve(first, act_at):
                step(nc.vector.tensor_reduce(st(0), h_all[:, :, :], AX.X, ALU.add))
                dve.wait_ge(a_dve, first)
                step(nc.vector.scalar_tensor_tensor(t3(b3), wide(0), -1.0 / D, h_all[:, :, :], ALU.mult, ALU.add))
                dve.wait_ge(a_act, act_at)
                step(nc.vector.tensor_reduce(st(3), t3(b4), AX.X, ALU.add))
                dve.wait_ge(a_dve, first + 2)
                step(nc.vector.tensor_scalar(st(1), st(3), 1.0 / D, EPS, ALU.mult, ALU.add))
                dve.wait_ge(a_act, act_at + 1)
                link(nc.vector.reciprocal(st(4), st(2)))

            norm_dve(10, 6)
            nc.vector.memset(stats[:, 7, :], 0.0).then_inc(h1_done, 1)
            xs = b6[:, 0:512].rearrange("p (t f) -> p t f", t=8)
            with dve.Fori(0, 8) as a:
                nc.vector.tensor_tensor(
                    xs, t3(b3)[:, bass.ds(a * 8, 8), :],
                    stats[:, 4, bass.ds(a * 8, 8)].unsqueeze(2).broadcast_to([128, 8, D]), ALU.mult).then_inc(xs_done, 1)
                dve.wait_ge(xw_pe, a + 1)
                nc.vector.tensor_copy(b4[0:D, 1024:2048].rearrange("p (c n) -> p c n", c=2), ybank[1][0:D])\
                    .then_inc(xw_dve, 1)
                for y in range(2):
                    dve.wait_ge(s_pe, 2 * a + y + 1)
                    nc.vector.tensor_reduce(
                        stats[:, 7, 4 * y:4 * y + 4],
                        ybank[y][:, :, :].rearrange("p c (t m) -> p (c t) m", t=2)[:, :, 0:NW],
                        AX.X, ALU.max, negate=True).then_inc(smax_link, 1)
                    dve.wait_ge(smax_link, 2 * a + y + 1)
                    nc.vector.tensor_scalar(stats[:, 5, 4 * y:4 * y + 4], stats[:, 7, 4 * y:4 * y + 4], 0.125, None,
                                            ALU.mult).then_inc(smax_done, 1)
                for i in range(2):
                    dve.wait_ge(pt_pe, 4 * a + i + 3)
                    nc.vector.tensor_copy(b2[:, 512 * (2 + i):512 * (3 + i)], bank[6 + i]).then_inc(pt_dve, 1)
                nc.vector.reciprocal(stats[:, 7, 8:16], stats[:, 6, 0:8]).then_inc(r_link, 1)
                dve.wait_ge(r_link, 2 * a + 1)
                dve.wait_ge(msg_pe, a + 1)
                nc.vector.tensor_tensor(b6[:, 1024:1536].rearrange("p (t f) -> p t f", t=8),
                                        ybank[0][:, 0, :].rearrange("p (t f) -> p t f", t=8),
                                        stats[:, 7, 8:16].unsqueeze(2).broadcast_to([128, 8, D]), ALU.mult)\
                    .then_inc(r_link, 1)
                dve.wait_ge(r_link, 2 * a + 2)
                hv = h_all[:, bass.ds(a * 8, 8), :]
                nc.vector.tensor_tensor(hv, hv, b6[:, 1024:1536].rearrange("p (t f) -> p t f", t=8), ALU.add)\
                    .then_inc(h1_done, 1)
            dve.wait_ge(h1_done, 9)
            norm_dve(14, 8)
            step(nc.vector.tensor_tensor(t3(b6), t3(b3), wide(4), ALU.mult))

            def slot(it, s):
                select, gather, attend = flags(it)
                if select:
                    select_wait(it + 1, s)
                pair = pair_of(it, s)
                if pair:
                    n, u, _own = pair
                    wait(dve, e_done, n + 1)
                    wait(dve, gather_done, n - 3)
                    nc.vector.scalar_tensor_tensor(wgt[:, u % 4, :, :], ybank[s % 2][:, :, :], 0.0, esum[:, s % 2, :, :],
                                                   ALU.is_ge, ALU.mult).then_inc(w_done, 1)
                if s == 0 and attend:
                    j = it - 1
                    wait(dve, kva_act, j + 1)
                    wait(dve, gather_done, PAIRS * (j + 1))
                    wait(dve, kvn_pe, j)
                    nc.vector.tensor_tensor(kv_t, acc[1][:, :], kv_a, ALU.add).then_inc(kvt_dve, 1)
                if s == 2 and attend:
                    j = it - 1
                    wait(dve, kvn_pe, j + 1)
                    wait(dve, rz_link, j + 1)
                    wait(dve, o_pe, j)
                    nc.vector.tensor_tensor(kv_n, misc[0][:, :].rearrange("p (t d) -> p t d", t=GT),
                                            rz[:, :].unsqueeze(2).broadcast_to([128, GT, 128]), ALU.mult)\
                        .then_inc(kvn_dve, 1)
                if s == 3 and gather:
                    wait(dve, select_step, SEL * it + SEL)
                    wait(dve, rzn_done, it + 1)
                    wait(dve, kvn_dve, it)
                    nc.vector.tensor_copy(rz[:, :], rz_new[:, :]).then_inc(rz_link, 1)
                if s in (9, 10) and attend:
                    j, x = it - 1, s - 9
                    wait(dve, sim_pe, 2 * j + x + 1)
                    nc.vector.tensor_tensor(simm[:, x, :], misc[x][:, 0:384], causal[:, :], ALU.add)\
                        .then_inc(sim_link, 1)
                    wait(dve, sim_link, 2 * j + x + 1)
                    nc.vector.tensor_reduce(nmax[:, 2 * x:2 * x + 1], simm[:, x, 0:128], AX.X, ALU.max, negate=True)\
                        .then_inc(simm_dve, 1)
                    nc.vector.tensor_reduce(nmax[:, 2 * x + 1:2 * x + 2], simm[:, x, 128:384], AX.X, ALU.max,
                                            negate=True).then_inc(simm_dve, 1)
                if s == 15 and attend:
                    j = it - 1
                    wait(dve, prob_act, 2 * j + 2)
                    nc.vector.reciprocal(rl[:, :], lsum[:, :]).then_inc(rl_link, 1)
                    wait(dve, rl_link, 2 * j + 1)
                    wait(dve, y_pe, j + 1)
                    nc.vector.tensor_tensor(y_n[:, :, :], misc[1][:, 0:256].rearrange("p (t f) -> p t f", t=GT),
                                            rl[:, :].unsqueeze(2).broadcast_to([128, GT, D]), ALU.mult)\
                        .then_inc(rl_link, 1)
                    wait(dve, rl_link, 2 * j + 2)
                    if static(j):
                        hv = h_all[:, GT * (j % GROUPS):GT * (j % GROUPS) + GT, :]
                    else:
                        hv = h_all[:, bass.ds((j % GROUPS) * GT, GT), :]
                    nc.vector.tensor_tensor(hv, hv, y_n[:, :, :], ALU.add).then_inc(h_dve, 1)
                if select:
                    select_part(it + 1, s)

            def select_wait(j, s):
                if s == 1:
                    wait(dve, score_act, j + 1)
                if 2 <= s <= 8:
                    wait(dve, select_step, SEL * j + (1, 2, 3, 4, 6, 8, 11)[s - 2])
                if s == 13:
                    wait(dve, wexp_act, j + 1)

            def hold(j, step):
                wait(dve, select_step, SEL * j + step)
                nc.vector.tensor_copy(gate[:, 0:1], gate[:, 1:2])

            def select_part(j, s):
                def done(ins):
                    ins.then_inc(select_step, 1)

                halves = [(t, p) for t in range(GT) for p in range(2)]
                if s == 1:
                    for t, p in halves:
                        last = nc.vector.max(top[:, t, p, 0:8], score[:, t, p, :])
                    done(last)
                if s == 2:
                    for t, p in halves:
                        last = nc.vector.match_replace(score_m[:, t, p, :], top[:, t, p, 0:8], score[:, t, p, :], LOW)
                    done(last)
                if s == 3:
                    for t, p in halves:
                        last = nc.vector.max(top[:, t, p, 8:16], score_m[:, t, p, :])
                    done(last)
                if s == 4:
                    at = 0
                    for lo, hi, n in CAND:
                        m = hi - lo
                        last = nc.vector.tensor_tensor(
                            cand[:, :, at:at + m * n].rearrange("p t (i k) -> p t i k", i=m),
                            top[:, :, 0, lo:hi].unsqueeze(3).broadcast_to([128, GT, m, n]),
                            top[:, :, 1, 0:n].unsqueeze(2).broadcast_to([128, GT, m, n]), ALU.add)
                        at += m * n
                    done(last)
                if s == 5:
                    for t in range(GT):
                        last = nc.vector.max(best[:, t, 0:8], cand[:, t, :])
                    done(last)
                    hold(j, 5)
                    for t in range(GT):
                        last = nc.vector.match_replace(cand_m[:, t, :], best[:, t, 0:8], cand[:, t, :], LOW)
                    done(last)
                if s == 6:
                    for t in range(GT):
                        last = nc.vector.max(best[:, t, 8:16], cand_m[:, t, :])
                    done(last)
                    hold(j, 7)
                    for t in range(GT):
                        last = nc.vector.match_replace(cand_mm[:, t, :], best[:, t, 8:16], cand_m[:, t, :], LOW)
                    done(last)
                if s == 7:
                    nc.vector.tensor_scalar(small[:, 2, :], best[:, :, 0], -SPREAD, None, ALU.add)
                    done(nc.vector.tensor_reduce(small[:, 0, :], cand_mm[:, :, :], AX.X, ALU.max))
                    wait(dve, select_step, SEL * j + 9)
                    done(nc.vector.tensor_tensor(small[:, 1, :], small[:, 0, :], best[:, :, 15], ALU.add))
                    wait(dve, select_step, SEL * j + 10)
                    done(nc.vector.scalar_tensor_tensor(small[:, 3, :], small[:, 1, :], 0.5, small[:, 2, :],
                                                        ALU.mult, ALU.max))
                if s == 8:
                    thr = small[:, 3, :].unsqueeze(2)
                    nc.vector.tensor_tensor(wsel[:, :, :], best[:, :, :], thr.broadcast_to([128, GT, TOPK]), ALU.subtract)
                    done(nc.vector.tensor_tensor(shifted, score[:, :, 1, :],
                                                 thr.broadcast_to([128, GT, NK]), ALU.subtract))
                    wait(dve, select_step, SEL * j + 12)
                    wait(dve, quad_pe, 4 * j)
                    for high, _low, src in PLACES:
                        last = nc.vector.tensor_scalar(high.bitcast(I32), src.bitcast(I32), HIGH_BITS, None,
                                                       ALU.bitwise_and)
                    done(last)
                if s == 13:
                    nc.vector.scalar_tensor_tensor(wbest[:, :, :], wsel[:, :, :], 0.0, wbest[:, :, :],
                                                   ALU.is_ge, ALU.mult).then_inc(rzn_link, 1)
                    wait(dve, rzn_link, 2 * j + 1)
                    nc.vector.tensor_reduce(small[:, 4, :], wbest[:, :, :], AX.X, ALU.add).then_inc(rzn_link, 1)
                    wait(dve, rzn_link, 2 * j + 2)
                    nc.vector.reciprocal(rz_new[:, :], small[:, 4, :]).then_inc(rzn_done, 1)

            def body(it):
                for s in range(PAIRS):
                    slot(it, s)

            run_iterations(dve, body)


def interpolation_weights():
    import numpy as np
    f = np.float32
    n = L
    count = int((n - 1) / 0.25) + 1
    step = np.arange(count - 1, dtype=f) * (f(1) / f(count - 1))
    x = np.concatenate([step, np.ones(1, f)]) * f(n - 1)
    x = np.concatenate([x, np.full(L * UP - count, x[-1], f)])
    i0 = np.floor(x).astype(np.int32)
    frac = x - i0.astype(f)
    a = f(-0.75)
    out = np.zeros((TAPS, L * UP), f)
    p = np.arange(L * UP)
    for off in range(-1, 3):
        at = np.abs(frac - f(off))
        near = ((a + f(2)) * at - (a + f(3))) * at * at + f(1)
        far = ((a * at - f(5) * a) * at + f(8) * a) * at - f(4) * a
        w = np.where(at <= 1, near, np.where(at < 2, far, f(0)))
        k = i0 + off - p // UP + 2
        ok = (k >= 0) & (k < TAPS)
        out[k[ok], p[ok]] += w[ok]
    return np.ascontiguousarray(out.reshape(TAPS, QUARTERS, PTS).transpose(1, 0, 2))


def dft_matrix():
    import numpy as np
    n = np.arange(WIN)
    ang = 2 * np.pi * (n[:, None] * n[None, :] % WIN) / WIN
    m = np.concatenate([np.cos(ang), np.sin(ang)], 1).astype(np.float32)
    return np.concatenate([m, m], 0)


def onehot_matrices():
    import numpy as np
    m = np.zeros((128, 8, 128), np.float32)
    for r in range(8):
        for jj in range(4):
            for ii in range(32):
                for k in (ii, 32 + ii, 64 + 4 * r + jj, 96 + 4 * r + jj):
                    m[k, r, 32 * jj + ii] = 1
    return m


def causal_mask():
    import numpy as np
    tri = np.where(np.arange(128)[:, None] >= np.arange(128)[None, :], 0, LOW).astype(np.float32)
    return np.concatenate([tri, np.zeros((128, 128), np.float32), tri], 1)


def kernel(x, L0_attn_W, L0_ffn_Wq_pk, L0_ffn_pk_keys, L0_ffn_Wq, L0_ffn_keys_table, L0_ffn_values_table, L0_ffn_Wo):
    import numpy as np
    import concourse.bacc as bacc
    from concourse.bass_utils import run_bass_kernel_spmd

    x = np.asarray(x)
    xp = np.concatenate([x[:, :1], x[:, :1], x, x[:, -1:], x[:, -1:]], 1)
    wqpk = np.asarray(L0_ffn_Wq_pk).reshape(D, 2, HEADS, 32).transpose(3, 2, 1, 0).reshape(32, 2 * HEADS, D)
    keys = np.asarray(L0_ffn_pk_keys).transpose(3, 2, 0, 1).reshape(32, 2 * HEADS, NK)
    kv = np.concatenate([np.asarray(L0_ffn_keys_table), np.asarray(L0_ffn_values_table)], 1)
    kv = kv.reshape(HEADS, 2, 8, 4, 2, 32, 2 * D).transpose(0, 3, 5, 4, 1, 2, 6).reshape(HEADS, 128, SLICES, 2 * D)
    wq = np.asarray(L0_ffn_Wq).reshape(D, HEADS, D).transpose(1, 0, 2)
    wo = np.asarray(L0_ffn_Wo).reshape(HEADS, D, D)
    qo = np.stack([wq, wo], 2)
    arrays = {
        "xp": xp, "interp_w": interpolation_weights(), "dft": dft_matrix(), "ident": np.eye(128, dtype=np.float32),
        "onehot": onehot_matrices(), "causal": causal_mask(), "attn_w": np.asarray(L0_attn_W), "wqpk_t": wqpk,
        "keys_t": keys, "table": kv, "qo_w": qo,
    }
    arrays = {"in_" + n: np.ascontiguousarray(a) for n, a in arrays.items()}
    nc = bacc.Bacc("TRN2", target_bir_lowering=False, num_devices=1)
    args = [nc.dram_tensor(n, a.shape, mybir.dt.from_np(a.dtype), kind="ExternalInput").ap() for n, a in arrays.items()]
    args.append(nc.dram_tensor("out", (B, NW, D), F32, kind="ExternalOutput").ap())
    program(nc, *args)
    r = run_bass_kernel_spmd(nc, [arrays], core_ids=[0])
    return r.results[0]["out"]
```

```python
from contextlib import ExitStack

import concourse.bass as bass
from concourse import mybir

F32 = mybir.dt.float32
F32R = mybir.dt.float32r
I32 = mybir.dt.int32
ACT = mybir.ActivationFunctionType
ALU = mybir.AluOpType
AX = mybir.AxisListType

B, L = 32, 4096
UP, WIN = 4, 64
NW = 255
NT = 256
D = 64
QUARTERS = 4
PTS = L * UP // QUARTERS
TAPS = 5
CH = 4
HEADS, NK, TOPK = 8, 64, 16
TILES = B * NT // 128
GT = 4
TOK = GT * 128
GROUPS = TILES // GT
ITERS = HEADS * GROUPS
SLICES = NK * NK // 128
PAIRS = SLICES // 2
LEAD = 5
WBUF, LBUF = 8, 4
PIECE = 4
PREP = 8
PIECES = SLICES // PIECE
CAND = [(0, 1, 16), (1, 2, 8), (2, 4, 5), (4, 8, 3), (8, 16, 1)]
NC = sum((hi - lo) * n for lo, hi, n in CAND)
EPS = 1e-5
LOW = -3.0e38
SPREAD = 120.0
EXP_SHIFT = -40.0
HIGH_BITS = -4096
QUADS = [(0, 0), (1, 0), (1, 1), (0, 1)]
DVE_HIGH = (2, 5, 9, 14)
DVE_LOW = (12,)


def program(nc, xp, interp_w, dft, ident_d, onehot_d, causal_d, attn_w, wqpk_t, keys_t, table, wq_d, wo_d, out):
    ctx = ExitStack()
    with ctx:
        def sb(name, shape, dt=F32):
            return ctx.enter_context(nc.sbuf_tensor(name, shape, dt))

        def sem(name):
            return ctx.enter_context(nc.semaphore(name))

        h0_dram = nc.dram_tensor("h0_scratch", (B, NT, D), F32, kind="Internal").ap()
        zt_dram = nc.dram_tensor("zt_scratch", (128, TILES, 128), F32, kind="Internal").ap()
        wq_dram = nc.dram_tensor("wq_scratch", (128, HEADS, 3 * D), F32, kind="Internal").ap()
        th_dram = nc.dram_tensor("t_high_scratch", (HEADS, 128, SLICES, 128), F32, kind="Internal").ap()
        tl_dram = nc.dram_tensor("t_low_scratch", (HEADS, 128, SLICES, 128), F32, kind="Internal").ap()

        h_all = sb("h_all", [128, TILES, D])
        ident = sb("ident", [128, 128])
        onehot = sb("onehot", [128, 2, 8, 128], F32R)
        causal = sb("causal", [128, 384])
        c_high = sb("c_high", [128, HEADS, 128], F32R)
        c_low = sb("c_low", [128, HEADS, 128], F32R)
        m40 = sb("m40", [128, 4])
        gate = sb("gate", [128, 2])

        with ExitStack() as phase_a:
            def sa(name, shape, dt=F32):
                return phase_a.enter_context(nc.sbuf_tensor(name, shape, dt))

            blk = [sa(f"block{i}", [128, 4096]) for i in range(2)]
            weights_sb = sa("interp_weights", [128, TAPS, PTS])
            stats = sa("stats", [128, 8, TILES])
            signal = sa("signal", [128, 1028])
            dft_sb = sa("dft_sb", [128, 128])
            wattn = sa("wattn", [D, 2, D])
            onehot_f = blk[1][:, 0:2048].rearrange("p (a r n) -> p a r n", a=2, r=8)
            pk_w = blk[1][0:32, 2048:4096].rearrange("p (i a d) -> p i a d", i=2 * HEADS, a=2)
            pk_k = blk[0][0:32, 0:1024].rearrange("p (i k) -> p i k", i=2 * HEADS)
            wq_f = blk[0][:, 1024:1536].rearrange("p (h d) -> p h d", h=HEADS)
            wq_parts = blk[0][:, 1536:3072].rearrange("p (h c d) -> p h c d", h=HEADS, c=3)
            prep_raw = sa("prep_raw", [128, 2, PREP * 128])
            prep_high = sa("prep_high", [128, 2, PREP * 128], F32R)
            prep_zero = sa("prep_zero", [128, 1])[:, :]
            prep_low = sa("prep_low", [128, 2, PREP * 128], F32R)
        blk += [weights_sb[:, i, :] for i in range(TAPS)]
        interp = blk[0][:, :]
        scr = blk[1][:, :]
        b2, b3, b4, b5, b6 = [blk[i] for i in range(2, 7)]
        z_parts = weights_sb[:, 0:2, :].rearrange("p a n -> p (a n)").rearrange("p (t c f) -> p t c f", c=2, f=D)
        zt_sb = weights_sb[:, 2:4, :].rearrange("p a n -> p (a n)").rearrange("p (t n) -> p t n", n=128)

        t_high = sb("t_high", [128, SLICES, 128], F32R)
        t_low = sb("t_low", [128, SLICES, 128], F32R)
        wgt = sb("wgt", [128, WBUF, 2, TOK])
        w_high = sb("w_high", [128, WBUF, 2, TOK], F32R)
        w_low = sb("w_low", [128, LBUF, 2, TOK], F32R)
        rsum = sb("rsum", [128, 4, TOK], F32R)
        z_sel = sb("z_sel", [128, TOK], F32R)
        z_att = sb("z_att", [128, TOK], F32R)
        wq = sb("wq", [128, 3 * D], F32R)
        wo = sb("wo", [D, D])
        score = sb("score", [128, GT, 2, NK])
        score_m = sb("score_m", [128, GT, 2, NK])
        shifted = sb("shifted", [128, GT, NK])
        parts = sb("parts", [128, GT, 5, 2, 32])
        top = sb("top", [128, GT, 2, TOPK])
        cand = sb("cand", [128, GT, NC])
        cand_m = sb("cand_m", [128, GT, NC])
        cand_mm = sb("cand_mm", [128, GT, NC])
        best = sb("best", [128, GT, TOPK])
        small = sb("small", [128, 8, GT])
        wbest = sb("wbest", [128, GT, TOPK])
        wsel = sb("wsel", [128, GT, TOPK])
        rz_new = sb("rz_new", [128, GT])
        rz = sb("rz", [128, GT])
        kv_a = sb("kv_a", [128, TOK])[:, :]
        kv_t = sb("kv_t", [128, TOK])[:, :]
        kv_n = sb("kv_n", [128, GT, 128])
        k_t = sb("k_t", [D, TOK])[:, :]
        q_t = sb("q_t", [D, TOK])[:, :]
        simm = sb("simm", [128, 2, 384])
        prob = sb("prob", [128, 2, 384])
        prob_t = sb("prob_t", [128, 2, 384])
        o_t = sb("o_t", [D, TOK])[:, :]
        nmax = sb("nmax", [128, 4])
        lsum = sb("lsum", [128, 4])
        rl = sb("rl", [128, 4])
        y_n = sb("y_n", [128, GT, D])

        ybank = [ctx.enter_context(nc.psum_tensor(f"ybank{i}", [128, 2, 512], F32)) for i in range(2)]
        acc = [ctx.enter_context(nc.psum_tensor(f"acc{i}", [128, 512], F32)) for i in range(2)]
        misc = [ctx.enter_context(nc.psum_tensor(f"misc{i}", [128, 512], F32)) for i in range(2)]
        bank = [ybank[0][:, 0, :], ybank[0][:, 1, :], ybank[1][:, 0, :], ybank[1][:, 1, :],
                acc[0][:, :], acc[1][:, :], misc[0][:, :], misc[1][:, :]]

        ld_small, ld_sig = sem("ld_small"), sem("ld_sig")
        ld_w = [sem(f"ld_w{c}") for c in range(CH)]
        const_ready = sem("const_ready")
        interp_done, squares_done, kw_done = sem("interp_done"), sem("squares_done"), sem("kw_done")
        kwt_pe, kwt_act = sem("kwt_pe"), sem("kwt_act")
        dft_pe, dft_act = sem("dft_pe"), sem("dft_act")
        a_dve, a_act = sem("a_dve"), sem("a_act")
        h0_stored, h0_loaded = sem("h0_stored"), sem("h0_loaded")
        xs_done, xt_pe, xt_act, xw_pe, xw_dve = (sem(n) for n in ("xs_done", "xt_pe", "xt_act", "xw_pe", "xw_dve"))
        s_pe, smax_done, p_act, pt_pe, pt_act, pt_dve, msg_pe, h1_done = (
            sem(n) for n in ("s_pe", "smax_done", "p_act", "pt_pe", "pt_act", "pt_dve", "msg_pe", "h1_done"))
        zt_pe, zt_act, zt_stored, ctab_pe, ctab_act = (
            sem(n) for n in ("zt_pe", "zt_act", "zt_stored", "ctab_pe", "ctab_act"))
        link_a = sem("link_a")
        z_sel_in, z_att_in, wq_in, wo_in = (sem(n) for n in ("z_sel_in", "z_att_in", "wq_in", "wo_in"))
        prep_in = [sem(f"prep_in{i}") for i in range(2)]
        prep_out = [sem(f"prep_out{i}") for i in range(2)]
        prep_zeroed = sem("prep_zeroed")
        prep_step, ctab_dve, wq_split, wq_stored = (
            sem(n) for n in ("prep_step", "ctab_dve", "wq_split", "wq_stored"))
        high_act, high_dve, low_pool_w, low_dve = (sem(n) for n in ("high_act", "high_dve", "low_pool_w", "low_dve"))
        tab_in = [sem(f"tab_in{p}") for p in range(PIECES)]
        scores_pe, score_act, select_step = sem("scores_pe"), sem("score_act"), sem("select_step")
        quad_pe, quad_act = sem("quad_pe"), sem("quad_act")
        y_done, e_done, w_done, gather_done = sem("y_done"), sem("e_done"), sem("w_done"), sem("gather_done")
        kva_act, kvt_dve, kvn_pe, kvn_dve = sem("kva_act"), sem("kvt_dve"), sem("kvn_pe"), sem("kvn_dve")
        q_pe, q_act, kt_pe, kt_act = sem("q_pe"), sem("q_act"), sem("kt_pe"), sem("kt_act")
        sim_pe, simm_dve, prob_act = sem("sim_pe"), sem("simm_dve"), sem("prob_act")
        probt_pe, probt_act, o_pe, o_act, y_pe, h_dve = (
            sem(n) for n in ("probt_pe", "probt_act", "o_pe", "o_act", "y_pe", "h_dve"))
        rz_link, out_stored = sem("rz_link"), sem("out_stored")
        smax_link, r_link, sim_link, rl_link, rzn_link, rzn_done = (
            sem(n) for n in ("smax_link", "r_link", "sim_link", "rl_link", "rzn_link", "rzn_done"))
        wexp_act, guard_dve = sem("wexp_act"), sem("guard_dve")

        SEL = 14
        QUAD_SLOTS = (9, 13, 15, 4)
        half0 = score[:, :, 0, :].rearrange("p t (a k) -> p t a k", a=2)
        half1 = shifted[:, :, :].rearrange("p t (a k) -> p t a k", a=2)
        PLACES = [(parts[:, :, 0:4:2, 0, :], parts[:, :, 0:4:2, 1, :], half0),
                  (parts[:, :, 1:4:2, 0, :], parts[:, :, 1:4:2, 1, :], half1),
                  (parts[:, :, 4, 0, :], parts[:, :, 4, 1, :], half0[:, :, 0, :])]
        LOADS = 11
        block = ctx.enter_context(nc.Block())

        def static(it):
            return isinstance(it, int)

        def flags(it):
            if not static(it):
                return True, True, True, True, True
            return it + 2 < ITERS, 0 <= it + 1 < ITERS, 0 <= it < ITERS, 1 <= it <= ITERS, it >= 2

        def quad_of(it, s):
            if s not in QUAD_SLOTS:
                return None
            quad = QUAD_SLOTS.index(s)
            j = it if quad == 3 else it + 1
            return (j, quad) if not static(it) or 0 <= j < ITERS else None

        def pair_of(it, s, lead=LEAD):
            owner = it if s + lead < PAIRS else it + 1
            if static(it) and not 0 <= owner < ITERS:
                return None
            return it * PAIRS + s + lead, (s + lead) % PAIRS, owner

        def before(it, u, back):
            return (it, u - back) if u >= back else (it - 1, u - back + PAIRS)

        def made(it, u, by_dve, dve_sem, other_sem):
            mine = [x for x in range(PAIRS) if (x in by_dve) == (u in by_dve)]
            return (dve_sem if u in by_dve else other_sem), it * len(mine) + mine.index(u) + 1

        def wait(eng, s, value):
            if static(value) and value <= 0:
                return
            eng.wait_ge(s, value)

        def run_iterations(eng, body):
            for it in (-2, -1, 0, 1):
                body(it)
            with eng.Fori(2, ITERS - 2) as it:
                body(it)
            for it in (ITERS - 2, ITERS - 1, ITERS, ITERS + 1):
                body(it)

        @block.sync
        def _(sp):
            sp.dma_start(ident[:, :], ident_d).then_inc(ld_small, 16)
            sp.dma_start(dft_sb[:, :], dft).then_inc(ld_small, 16)
            sp.dma_start(onehot_f, onehot_d).then_inc(ld_small, 16)
            sp.dma_start(causal[:, :], causal_d).then_inc(ld_small, 16)
            for i in range(2):
                sp.dma_start(wattn[:, i, :], attn_w).then_inc(ld_small, 16)
                sp.dma_start(pk_w[:, :, i, :], wqpk_t).then_inc(ld_small, 16)
                sp.dma_start(wq_f[64 * i:64 * i + 64], wq_d).then_inc(ld_small, 16)
            sp.dma_start(pk_k, keys_t).then_inc(ld_small, 16)
            sp.wait_ge(wq_split, 3)
            sp.dma_start(wq_dram.rearrange("p h n -> p (h n)"), wq_parts.rearrange("p h c d -> p (h c d)"))\
              .then_inc(wq_stored, 16)
            sp.wait_ge(a_dve, 8)
            for q in range(QUARTERS):
                sp.dma_start(h0_dram[:, q * 64:(q + 1) * 64, :],
                             interp[32 * q:32 * q + 32, :].rearrange("b (w f) -> b w f", w=64)).then_inc(h0_stored, 16)
            sp.wait_ge(h0_stored, 16 * QUARTERS)
            sp.dma_start(h_all[:, 0:TILES // 2, :],
                         h0_dram[0:B // 2].rearrange("b (nh p) f -> p (b nh) f", p=128)).then_inc(h0_loaded, 16)
            sp.dma_start(h_all[:, TILES // 2:TILES, :],
                         h0_dram[B // 2:B].rearrange("b (nh p) f -> p (b nh) f", p=128)).then_inc(h0_loaded, 16)
            for g in range(4):
                c = slice(TILES // 4 * g, TILES // 4 * (g + 1))
                sp.wait_ge(zt_act, 4 * (g + 1))
                sp.dma_start(zt_dram[:, c, :], zt_sb[:, c, :]).then_inc(zt_stored, 16)
            sp.wait_ge(zt_stored, 16 * 4)
            sp.wait_ge(wq_stored, 16)
            for i in range(2):
                sp.wait_ge(prep_out[i], 32 * HEADS * SLICES // PREP // 2)

            def load_select(j, g):
                wait(sp, scores_pe, j)
                sp.dma_start(z_sel[:, :].bitcast(F32).rearrange("d (t n) -> d t n", t=GT),
                             zt_dram[:, bass.ds(g * GT, GT), :]).then_inc(z_sel_in, 16)

            def load_query(j, g, h):
                wait(sp, q_pe, j)
                sp.dma_start(z_att[:, :].bitcast(F32).rearrange("d (t n) -> d t n", t=GT),
                             zt_dram[:, bass.ds(g * GT, GT), :]).then_inc(z_att_in, 16)
                sp.dma_start(wq[:, :].bitcast(F32), wq_dram[:, bass.ds(h, 1), :].rearrange("p a n -> p (a n)"))\
                    .then_inc(wq_in, 16)

            def load_wo(j, h):
                wait(sp, y_pe, j)
                sp.dma_start(wo[:, :], wo_d[bass.ds(h, 1)].rearrange("a d n -> (a d) n")).then_inc(wo_in, 16)

            def load_table(h):
                for p in range(PIECES):
                    wait(sp, gather_done, h * GROUPS * PAIRS - PAIRS + 2 * (p + 1))
                    for dst, src in ((t_high, th_dram), (t_low, tl_dram)):
                        sp.dma_start(dst[:, p * PIECE:(p + 1) * PIECE, :].bitcast(F32),
                                     src[bass.ds(h, 1), :, p * PIECE:(p + 1) * PIECE, :]
                                     .rearrange("a p c n -> (a p) c n")).then_inc(tab_in[p], 16)

            load_select(0, 0)
            load_table(0)
            load_select(1, 1)
            load_select(2, 2)
            load_query(0, 0, 0)

            def head_steps(h, first, end):
                with sp.Fori(first, end) as g:
                    load_select(h * GROUPS + g + 2, (g + 2) % GROUPS)
                    load_wo(h * GROUPS + g - 1, h)
                    load_query(h * GROUPS + g, g, h)

            def head_change(h):
                n = h * GROUPS
                load_select(n + 2, 2)
                load_wo(n - 1, h - 1)
                load_query(n, 0, h)

            head_steps(0, 1, GROUPS)
            load_table(1)
            with sp.Fori(1, HEADS - 1) as h:
                head_change(h)
                head_steps(h, 1, GROUPS)
                load_table(h + 1)
            last_head = HEADS - 1
            head_change(last_head)
            head_steps(last_head, 1, GROUPS - 2)
            for g in (GROUPS - 2, GROUPS - 1):
                load_wo(last_head * GROUPS + g - 1, last_head)
                load_query(last_head * GROUPS + g, g, last_head)
            load_wo(ITERS - 1, last_head)
            sp.wait_ge(h_dve, ITERS)
            hv = h_all[:, :, :].rearrange("p (b o) f -> p b o f", o=2)
            sp.dma_start(out[:, 0:128, :].rearrange("b p f -> p b f"), hv[:, :, 0, :]).then_inc(out_stored, 16)
            sp.dma_start(out[:, 128:NW, :].rearrange("b p f -> p b f"), hv[0:NW - 128, :, 1, :]).then_inc(out_stored, 16)
            sp.wait_ge(out_stored, 32)

        @block.gpsimd
        def _(pool):
            for s in range(QUARTERS):
                pool.dma_start(signal[32 * s:32 * s + 32, :], xp[:, 1024 * s:1024 * s + 1028]).then_inc(ld_sig, 16)
            for c in range(CH):
                for s in range(QUARTERS):
                    pool.dma_start(weights_sb[32 * s:32 * s + 32, :, 1024 * c:1024 * (c + 1)],
                                   interp_w[s, :, 1024 * c:1024 * (c + 1)].partition_broadcast(32)).then_inc(ld_w[c], 16)

            halves = SLICES // PREP // 2
            nc.gpsimd.memset(prep_zero, 0.0).then_inc(prep_zeroed, 1)
            pool.wait_ge(prep_zeroed, 1)

            def load_prep(h, k, b):
                pool.dma_start(prep_raw[:, b, :].rearrange("p (c n) -> p c n", n=128),
                               table[bass.ds(h, 1), :, bass.ds((2 * k + b) * PREP, PREP), :]
                               .rearrange("a p c n -> (a p) c n")).then_inc(prep_in[b], 16)

            def prep_body(h, k, i, first):
                for b in range(2):
                    pool.wait_ge(prep_in[b], 16 * (i + 1))
                    if not first:
                        pool.wait_ge(prep_out[b], 32 * i)
                    nc.gpsimd.tensor_tensor(prep_high[:, b, :], prep_raw[:, b, :],
                                            prep_zero.broadcast_to([128, PREP * 128]), ALU.add).then_inc(prep_step, 1)
                    pool.wait_ge(prep_step, 4 * i + 2 * b + 1)
                    nc.gpsimd.tensor_tensor(prep_low[:, b, :], prep_raw[:, b, :], prep_high[:, b, :].bitcast(F32),
                                            ALU.subtract).then_inc(prep_step, 1)
                    pool.wait_ge(prep_step, 4 * i + 2 * b + 2)
                    for dst, src in ((th_dram, prep_high), (tl_dram, prep_low)):
                        pool.dma_start(dst[bass.ds(h, 1), :, bass.ds((2 * k + b) * PREP, PREP), :]
                                       .rearrange("a p c n -> (a p) c n"),
                                       src[:, b, :].bitcast(F32).rearrange("p (c n) -> p c n", n=128))\
                            .then_inc(prep_out[b], 16)
                    nk = i + 1
                    if not (static(i) and i == HEADS * halves - 1):
                        load_prep(nk // halves, nk % halves, b)

            steps = HEADS * halves
            for b in range(2):
                load_prep(0, 0, b)
            prep_body(0, 0, 0, True)
            with pool.Fori(1, steps - 1) as i:
                prep_body(i // halves, i % halves, i, False)
            prep_body(HEADS - 1, halves - 1, steps - 1, False)

            def body(it):
                for s in range(PAIRS):
                    pair = pair_of(it, s)
                    if not pair or pair[1] in DVE_LOW:
                        continue
                    n, u, own = pair
                    wait(pool, *made(own, u, DVE_HIGH, high_dve, high_act))
                    wait(pool, gather_done, n - LBUF + 1)
                    nc.gpsimd.tensor_tensor(w_low[:, u % LBUF, :, :], wgt[:, u % WBUF, :, :],
                                            w_high[:, u % WBUF, :, :].bitcast(F32), ALU.subtract).then_inc(low_pool_w, 1)

            run_iterations(pool, body)

        @block.scalar
        def _(act):
            act.wait_ge(ld_small, 16 * LOADS)
            nc.scalar.activation(onehot[:, :, :, :], onehot_f, ACT.Copy).then_inc(const_ready, 1)
            act.wait_ge(ctab_pe, 1)
            for i in range(2):
                nc.scalar.activation(c_high[:, 4 * i:4 * i + 4, :],
                                     ybank[0][:, i, :].rearrange("p (h n) -> p h n", h=4), ACT.Copy)\
                  .then_inc(ctab_act, 1)
            act.wait_ge(guard_dve, 1)
            for c in range(CH):
                sl = slice(1024 * c, 1024 * (c + 1))
                act.wait_ge(interp_done, c + 1)
                nc.scalar.activation(scr[:, sl], interp[:, sl], ACT.Square, bias=m40[:, 1:2]).then_inc(squares_done, 1)
                act.wait_ge(squares_done, 3 * c + 1)
                nc.scalar.activation(weights_sb[:, 0, sl], scr[:, sl], ACT.Exp, scale=-0.5).then_inc(squares_done, 1)
                nc.scalar.activation(weights_sb[:, 1, sl], interp[:, sl], ACT.Square, bias=m40[:, 2:3])\
                    .then_inc(squares_done, 1)
            for g in range(8):
                act.wait_ge(kwt_pe, g + 1)
                nc.scalar.activation(b4[:, 512 * g:512 * (g + 1)], bank[g], ACT.Copy).then_inc(kwt_act, 1)
            for g in range(16):
                dst = (b2 if g < 8 else b3)[:, 512 * (g % 8):512 * (g % 8) + 512]
                act.wait_ge(dft_pe, g + 1)
                nc.scalar.activation(dst, bank[g % 8], ACT.Square).then_inc(dft_act, 1)
            act.wait_ge(a_dve, 1)
            nc.scalar.activation(b6, b5, ACT.Sqrt).then_inc(a_act, 1)
            act.wait_ge(a_dve, 3)
            nc.scalar.activation(b3, b2, ACT.Sigmoid).then_inc(a_act, 1)
            act.wait_ge(a_dve, 5)
            nc.scalar.activation(b3, b2, ACT.Abs).then_inc(a_act, 1)
            act.wait_ge(a_act, 3)
            nc.scalar.activation(b5, b3, ACT.Exp, scale=-1.0).then_inc(a_act, 1)
            act.wait_ge(a_act, 4)
            nc.scalar.activation(b4, b5, ACT.Ln, bias=1.0).then_inc(a_act, 1)

            def norm_act(dve_at, act_at):
                act.wait_ge(a_dve, dve_at)
                nc.scalar.activation(b4, b3, ACT.Square).then_inc(a_act, 1)
                act.wait_ge(a_dve, dve_at + 2)
                nc.scalar.activation(stats[:, 2, :], stats[:, 1, :], ACT.Sqrt).then_inc(a_act, 1)

            norm_act(11, 5)
            with act.Fori(0, 8) as a:
                act.wait_ge(xt_pe, a + 1)
                nc.scalar.activation(b4[0:D, 0:1024].rearrange("p (c n) -> p c n", c=2), ybank[0][0:D], ACT.Copy)\
                    .then_inc(xt_act, 1)
                for y in range(2):
                    act.wait_ge(smax_done, 2 * a + y + 1)
                    for t in range(4):
                        last = nc.scalar.activation(
                            b5[:, (4 * y + t) * 256:(4 * y + t) * 256 + NW],
                            ybank[y][:, t // 2, (t % 2) * 256:(t % 2) * 256 + NW],
                            ACT.Exp, bias=stats[:, 5, 4 * y + t:4 * y + t + 1], scale=0.125,
                            accum_out=stats[:, 6, 4 * y + t:4 * y + t + 1])
                    last.then_inc(p_act, 1)
                for i in range(2):
                    act.wait_ge(pt_pe, 4 * a + i + 1)
                    nc.scalar.activation(b2[:, 512 * i:512 * (i + 1)], bank[4 + i], ACT.Copy).then_inc(pt_act, 1)
            norm_act(15, 7)
            for g in range(16):
                act.wait_ge(zt_pe, g + 1)
                nc.scalar.activation(zt_sb[:, 4 * g:4 * g + 4, :], bank[g % 8].rearrange("p (t n) -> p t n", n=128),
                                     ACT.Copy).then_inc(zt_act, 1)

            def slot(it, s):
                starts, select, gather, attend, finish = flags(it)
                pair = pair_of(it, s)
                if pair:
                    n, u, own = pair
                    if not (static(n) and n < WBUF):
                        wait(act, *made(*before(own, u, WBUF), DVE_LOW, low_dve, low_pool_w))
                    wait(act, y_done, n + 1)
                    nc.scalar.activation(wgt[:, u % WBUF, :, :], ybank[s % 2][:, :, :], ACT.Exp,
                                         bias=m40[:, 0:1]).then_inc(e_done, 1)
                if s == 10 and starts:
                    j = it + 2
                    wait(act, scores_pe, j + 1)
                    wait(act, select_step, SEL * j)
                    nc.scalar.activation(score[:, :, :, :], misc[1][:, :].rearrange("p (t s k) -> p t s k", t=GT, s=2),
                                         ACT.Copy).then_inc(score_act, 1)
                prev = pair_of(it, s, LEAD - 1)
                if prev and prev[1] not in DVE_HIGH:
                    n, u, own = prev
                    wait(act, w_done, n + 1)
                    wait(act, gather_done, n - WBUF + 1)
                    nc.scalar.activation(w_high[:, u % WBUF, :, :], wgt[:, u % WBUF, :, :], ACT.Copy).then_inc(high_act, 1)
                if s == 3 and attend:
                    j = it - 1
                    wait(act, q_pe, j + 1)
                    nc.scalar.activation(q_t, misc[1][0:D, :], ACT.Copy, scale=0.125).then_inc(q_act, 1)
                if s == 5 and attend:
                    j = it - 1
                    wait(act, kt_pe, j + 1)
                    nc.scalar.activation(k_t, misc[1][0:D, :], ACT.Copy).then_inc(kt_act, 1)
                if s == 8 and gather:
                    wait(act, gather_done, PAIRS * it + PAIRS // 2)
                    wait(act, kvt_dve, it)
                    nc.scalar.activation(kv_a, acc[0][:, :], ACT.Copy).then_inc(kva_act, 1)
                if s in (9, 10) and attend:
                    j, x = it - 1, s - 9
                    wait(act, simm_dve, 4 * j + 2 * x + 2)
                    wait(act, h_dve, j)
                    nc.scalar.activation(prob[:, x, 0:128], simm[:, x, 0:128], ACT.Exp,
                                         bias=nmax[:, 2 * x:2 * x + 1], accum_out=lsum[:, 2 * x:2 * x + 1])
                    nc.scalar.activation(prob[:, x, 128:384], simm[:, x, 128:384], ACT.Exp,
                                         bias=nmax[:, 2 * x + 1:2 * x + 2],
                                         accum_out=lsum[:, 2 * x + 1:2 * x + 2]).then_inc(prob_act, 1)
                if s in (11, 12) and attend:
                    j, x = it - 1, s - 11
                    wait(act, probt_pe, 2 * j + x + 1)
                    nc.scalar.activation(prob_t[:, x, :], misc[x][:, 0:384], ACT.Copy).then_inc(probt_act, 1)
                if s == 14 and attend:
                    j = it - 1
                    wait(act, o_pe, j + 1)
                    nc.scalar.activation(o_t, misc[1][0:D, :], ACT.Copy).then_inc(o_act, 1)
                if quad_of(it, s):
                    j, quad = quad_of(it, s)
                    wait(act, y_done, PAIRS * (j - 1) + 4 * (quad + 1))
                    wait(act, quad_pe, 4 * j + quad + 1)
                    nc.scalar.activation(rsum[:, quad, :], misc[0][:, :], ACT.Copy).then_inc(quad_act, 1)
                if s == 7 and select:
                    j = it + 1
                    wait(act, select_step, SEL * j + 12)
                    nc.scalar.activation(wbest[:, :, :], wsel[:, :, :], ACT.Exp, bias=m40[:, 0:1]).then_inc(wexp_act, 1)

            def body(it):
                for s in range(PAIRS):
                    slot(it, s)

            run_iterations(act, body)

        @block.tensor
        def _(pe):
            pe.wait_ge(ld_small, 16 * LOADS)
            for h in range(HEADS):
                for half in range(2):
                    i = 2 * h + half
                    last = nc.tensor.matmul(ybank[0][:, h // 4, (h % 4) * 128 + 64 * half:(h % 4) * 128 + 64 * half + 64],
                                            pk_w[:, i].rearrange("p a d -> p (a d)"), pk_k[:, i, :], start=True, stop=True)
            last.then_inc(ctab_pe, 1)
            pe.wait_ge(ctab_dve, 2)
            for g in range(8):
                pe.wait_ge(kw_done, g // 2 + 1)
                for i in range(4):
                    c = (4 * g + i) * 128
                    last = nc.tensor.transpose(bank[g][:, 128 * i:128 * i + 128], b5[:, c:c + 128], ident[:, :])
                last.then_inc(kwt_pe, 1)
            kwt = b4.rearrange("p (w n) -> p w n", n=128)
            for g in range(16):
                pe.wait_ge(kwt_act, max(g // 2 + 1, g + 1 if g < 8 else 8))
                if g >= 8:
                    pe.wait_ge(dft_act, g - 7)
                for i in range(4):
                    w = 8 * (g // 2) + 2 * i + g % 2
                    lo = 64 * (w % 2)
                    last = nc.tensor.matmul(bank[g % 8][:, 128 * i:128 * i + 128], kwt[lo:lo + 64, w // 2, :],
                                            dft_sb[lo:lo + 64, :], start=True, stop=True)
                last.then_inc(dft_pe, 1)
            pe.wait_ge(dft_act, 16)
            xs = b6[:, 0:512].rearrange("p (t f) -> p t f", t=8)
            with pe.Fori(0, 8) as a:
                pe.wait_ge(xs_done, a + 1)
                pe.wait_ge(h1_done, a + 1)
                for t in range(8):
                    last = nc.tensor.transpose(ybank[0][:, t // 4, (t % 4) * 128:(t % 4) * 128 + 128],
                                               b6[:, 64 * t:64 * t + 128], ident[:, :])
                last.then_inc(xt_pe, 1)
                pe.wait_ge(xt_act, a + 1)
                for i in range(2):
                    last = nc.tensor.matmul(ybank[1][:, i, :], wattn[:, :, :].rearrange("p a n -> p (a n)"), b4[0:D, 512 * i:512 * (i + 1)],
                                            start=True, stop=True)
                last.then_inc(xw_pe, 1)
                pe.wait_ge(xw_dve, a + 1)
                for y in range(2):
                    for t in range(4):
                        tile = 4 * y + t
                        last = nc.tensor.matmul(ybank[y][:, t // 2, (t % 2) * 256:(t % 2) * 256 + NW],
                                                b4[0:D, 1024 + 128 * tile:1024 + 128 * tile + 128],
                                                b4[0:D, 256 * (tile // 2):256 * (tile // 2) + NW],
                                                start=True, stop=True)
                    last.then_inc(s_pe, 1)
                for t in range(8):
                    if t % 4 == 0:
                        pe.wait_ge(p_act, 2 * a + t // 4 + 1)
                    for mh in range(2):
                        last = nc.tensor.transpose(
                            bank[4 + t // 2][:, (2 * (t % 2) + mh) * 128:(2 * (t % 2) + mh) * 128 + 128],
                            b5[:, t * 256 + 128 * mh:t * 256 + 128 * mh + 128], ident[:, :])
                    if t % 2:
                        last.then_inc(pt_pe, 1)
                pe.wait_ge(pt_act, 2 * a + 2)
                pe.wait_ge(pt_dve, 2 * a + 2)
                for t in range(8):
                    for mh in range(2):
                        c = (2 * t + mh) * 128
                        last = nc.tensor.matmul(ybank[0][:, 0, 64 * t:64 * t + 64], b2[:, c:c + 128],
                                                xs[:, 2 * (t // 2) + mh, :], start=(mh == 0), stop=(mh == 1))
                last.then_inc(msg_pe, 1)
            for g in range(16):
                pe.wait_ge(a_dve, 20 + 3 * (g // 4))
                if g >= 8:
                    pe.wait_ge(zt_act, g - 7)
                for i in range(4):
                    last = nc.tensor.transpose(bank[g % 8][:, 128 * i:128 * i + 128],
                                               z_parts[:, 4 * g + i].rearrange("p c f -> p (c f)"), ident[:, :])
                last.then_inc(zt_pe, 1)
            pe.wait_ge(zt_act, 16)

            def slot(it, s):
                starts, select, gather, attend, finish = flags(it)
                pair = pair_of(it, s)
                if pair:
                    n, u, own = pair
                    wait(pe, w_done, n - 1)
                    quad = u // 4
                    if u % 4 == 0:
                        wait(pe, quad_act, 4 * own + quad + 1)
                    for c in range(2):
                        last = nc.tensor.matmul(ybank[s % 2][:, c, :], onehot[:, quad % 2, (2 * u + c) % 8, :],
                                                rsum[:, quad, :], start=True, stop=True)
                    last.then_inc(y_done, 1)
                if s == 0 and finish:
                    j = it - 2
                    wait(pe, wo_in, 16 * (j + 1))
                    wait(pe, o_act, j + 1)
                    for t in range(GT):
                        last = nc.tensor.matmul(misc[1][:, 64 * t:64 * t + 64], o_t[:, 128 * t:128 * t + 128],
                                                wo[:, :], start=True, stop=True)
                    last.then_inc(y_pe, 1)
                if s == 2 and attend:
                    j = it - 1
                    wait(pe, quad_act, min(4 * it + 3, 4 * ITERS) if static(it) else 4 * it + 3)
                    wait(pe, kvt_dve, j + 1)
                    for t in range(GT):
                        last = nc.tensor.transpose(misc[0][:, 128 * t:128 * t + 128], kv_t[:, 128 * t:128 * t + 128],
                                                   ident[:, :])
                    last.then_inc(kvn_pe, 1)
                if s == 3 and attend:
                    j = it - 1
                    wait(pe, wq_in, 16 * (j + 1))
                    wait(pe, z_att_in, 16 * (j + 1))
                    if static(it):
                        wait(pe, score_act, min(it + 2, ITERS))
                    wait(pe, rl_link, 2 * j)
                    for i in range(2):
                        last = nc.tensor.matmul(misc[1][:, :], wq[:, D * i:D * i + 2 * D], z_att[:, :],
                                                start=(i == 0), stop=(i == 1))
                    last.then_inc(q_pe, 1)
                if s == 5 and attend:
                    j = it - 1
                    wait(pe, kvn_dve, j + 1)
                    wait(pe, q_act, j + 1)
                    for t in range(GT):
                        last = nc.tensor.transpose(misc[1][:, 128 * t:128 * t + 128], kv_n[:, t, :], ident[:, :])
                    last.then_inc(kt_pe, 1)
                if quad_of(it, s):
                    j, quad = quad_of(it, s)
                    if quad == 0:
                        wait(pe, select_step, SEL * j + SEL)
                    if attend and quad == 0:
                        wait(pe, simm_dve, 4 * (it - 1) + 2)
                    if attend and quad == 1:
                        wait(pe, probt_act, 2 * (it - 1) + 1)
                    if attend and quad == 3:
                        wait(pe, kvn_dve, it)
                    wait(pe, quad_act, 4 * j + quad)
                    for t in range(GT):
                        src = parts[:, t, quad:quad + 2].rearrange("p q c k -> p (q c k)")
                        last = nc.tensor.transpose(misc[0][:, 128 * t:128 * t + 128], src, ident[:, :])
                    last.then_inc(quad_pe, 1)
                if s in (7, 8) and attend:
                    j, x = it - 1, s - 7
                    if x == 0:
                        wait(pe, quad_act, min(4 * it + 4, 4 * ITERS) if static(it) else 4 * it + 4)
                    wait(pe, kt_act, j + 1)
                    c = 256 * x
                    nc.tensor.matmul(misc[x][:, 0:128], q_t[:, c:c + 128], k_t[:, c:c + 128], start=True, stop=True)
                    nc.tensor.matmul(misc[x][:, 128:384], q_t[:, c + 128:c + 256], k_t[:, c:c + 256],
                                     start=True, stop=True).then_inc(sim_pe, 1)
                if s == 10 and starts:
                    j = it + 2
                    wait(pe, z_sel_in, 16 * (j + 1))
                    wait(pe, score_act, j)
                    if attend:
                        wait(pe, simm_dve, 4 * (it - 1) + 4)
                    for t in range(GT):
                        for i, c in enumerate((c_high, c_low)):
                            last = nc.tensor.matmul(misc[1][:, 128 * t:128 * t + 128], z_sel[:, 128 * t:128 * t + 128],
                                                    c[:, bass.ds(j // GROUPS, 1), :].rearrange("p a n -> p (a n)"),
                                                    start=(i == 0), stop=(i == 1))
                    last.then_inc(scores_pe, 1)
                if s in (11, 12) and attend:
                    j, x = it - 1, s - 11
                    if x == 0 and select:
                        wait(pe, quad_act, 4 * (it + 1) + 1)
                    if x == 1 and starts:
                        wait(pe, score_act, it + 3)
                    wait(pe, prob_act, 2 * j + x + 1)
                    for i in range(3):
                        last = nc.tensor.transpose(misc[x][:, 128 * i:128 * i + 128],
                                                   prob[:, x, 128 * i:128 * i + 128], ident[:, :])
                    last.then_inc(probt_pe, 1)
                if s == 14 and attend:
                    j = it - 1
                    wait(pe, probt_act, 2 * j + 2)
                    for x in range(2):
                        c = 256 * x
                        nc.tensor.matmul(misc[1][0:D, c:c + 256], kv_n[:, 2 * x, D:2 * D], prob_t[:, x, 0:256],
                                         start=True, stop=False)
                        last = nc.tensor.matmul(misc[1][0:D, c + 128:c + 256], kv_n[:, 2 * x + 1, D:2 * D],
                                                prob_t[:, x, 256:384], start=False, stop=True)
                    last.then_inc(o_pe, 1)
                if gather:
                    wait(pe, *made(it, s, DVE_LOW, low_dve, low_pool_w))
                    if s % 2 == 0:
                        wait(pe, tab_in[s // 2], 32 * (it // GROUPS + 1))
                    if s == 0:
                        wait(pe, kva_act, it)
                    if s == PAIRS // 2:
                        wait(pe, kvt_dve, it)
                    half = s // (PAIRS // 2)
                    for c in range(2):
                        k = 2 * s + c
                        for i, (t, w) in enumerate(((t_high, w_high), (t_high, w_low), (t_low, w_high))):
                            last = nc.tensor.matmul(acc[half][:, :], t[:, k, :], w[:, s % (LBUF if w is w_low else WBUF), c, :],
                                                    start=(k % (SLICES // 2) == 0 and i == 0),
                                                    stop=(k % (SLICES // 2) == SLICES // 2 - 1 and i == 2))
                    last.then_inc(gather_done, 1)

            def body(it):
                for s in range(PAIRS):
                    slot(it, s)

            run_iterations(pe, body)

        @block.vector
        def _(dve):
            steps = [0]

            def link(ins):
                steps[0] += 1
                ins.then_inc(link_a, 1)
                dve.wait_ge(link_a, steps[0])

            nc.vector.memset(gate[:, :], 0.0)
            nc.vector.memset(m40[:, 0:1], EXP_SHIFT)
            nc.vector.memset(m40[:, 1:2], -0.7)
            nc.vector.memset(m40[:, 2:3], 1.3).then_inc(guard_dve, 1)
            dve.wait_ge(ld_small, 16 * LOADS)
            for c in range(3):
                if c == 1:
                    dve.wait_ge(wq_split, 1)
                    nc.vector.tensor_tensor(wq_parts[:, :, 1, :], wq_f, wq_parts[:, :, 0, :], ALU.subtract)\
                        .then_inc(wq_split, 1)
                else:
                    nc.vector.tensor_scalar(wq_parts[:, :, c, :].bitcast(I32), wq_f.bitcast(I32), HIGH_BITS, None,
                                            ALU.bitwise_and).then_inc(wq_split, 1)
            for i in range(2):
                dve.wait_ge(ctab_act, 2)
                nc.vector.tensor_tensor(c_low[:, 4 * i:4 * i + 4, :], ybank[0][:, i, :].rearrange("p (h n) -> p h n", h=4),
                                        c_high[:, 4 * i:4 * i + 4, :].bitcast(F32), ALU.subtract).then_inc(ctab_dve, 1)
            dve.wait_ge(wq_stored, 16)
            dve.wait_ge(const_ready, 1)
            dve.wait_ge(ld_sig, 16 * QUARTERS)

            def kernels(c):
                sl = slice(1024 * c, 1024 * (c + 1))
                dve.wait_ge(squares_done, 3 * c + 3)
                link(nc.vector.tensor_tensor(weights_sb[:, 2, sl], weights_sb[:, 0, sl], weights_sb[:, 1, sl], ALU.add))
                nc.vector.tensor_scalar(b5[:, sl], weights_sb[:, 2, sl], 0.5, None, ALU.mult).then_inc(kw_done, 1)

            for c in range(CH):
                dve.wait_ge(ld_w[c], 16 * QUARTERS)

                def v(ap):
                    return ap[:, 1024 * c:1024 * (c + 1)].rearrange("p (s f) -> p s f", f=UP)

                def x(k):
                    return signal[:, 256 * c + k:256 * c + k + 256].unsqueeze(2).broadcast_to([128, 256, UP])

                link(nc.vector.tensor_tensor(v(interp), v(blk[2]), x(0), ALU.mult))
                for k in range(1, TAPS):
                    link(nc.vector.tensor_tensor(v(scr), v(blk[2 + k]), x(k), ALU.mult))
                    last = nc.vector.tensor_tensor(v(interp), v(interp), v(scr), ALU.add)
                    if k < TAPS - 1:
                        link(last)
                last.then_inc(interp_done, 1)
                if c >= 1:
                    kernels(c - 1)
            kernels(CH - 1)

            t3 = lambda ap: ap.rearrange("p (t f) -> p t f", f=D)
            st = lambda i: stats[:, i, :]
            wide = lambda i: stats[:, i, :].unsqueeze(2).broadcast_to([128, TILES, D])

            def step(ins):
                ins.then_inc(a_dve, 1)

            for g in range(2):
                dve.wait_ge(dft_act, 8 * (g + 1))
                sq = (b2, b3)[g].rearrange("p (c o i r f) -> p c o i r f", c=4, o=2, i=4, r=2)
                for o in range(2):
                    last = nc.vector.tensor_tensor(
                        b5[:, 2048 * g:2048 * (g + 1)].rearrange("p (c i o f) -> p c o i f", c=4, i=4, o=2)[:, :, o],
                        sq[:, :, o, :, 0, :], sq[:, :, o, :, 1, :], ALU.add)
            step(last)
            dve.wait_ge(a_act, 1)
            step(nc.vector.tensor_reduce(st(0), t3(b6), AX.X, ALU.max))
            dve.wait_ge(a_dve, 2)
            step(nc.vector.scalar_tensor_tensor(t3(b2), wide(0), -0.12, t3(b6), ALU.mult, ALU.add))
            dve.wait_ge(a_act, 2)
            step(nc.vector.tensor_tensor(b4, b6, b3, ALU.mult))
            dve.wait_ge(a_dve, 4)
            step(nc.vector.scalar_tensor_tensor(t3(b2), wide(0), -0.9, t3(b4), ALU.mult, ALU.add))
            dve.wait_ge(a_dve, 5)
            step(nc.vector.tensor_scalar(b6, b2, 0.0, None, ALU.min))
            dve.wait_ge(a_dve, 6)
            step(nc.vector.scalar_tensor_tensor(t3(b6), wide(0), 0.9, t3(b6), ALU.mult, ALU.add))
            dve.wait_ge(a_act, 5)
            dve.wait_ge(a_dve, 7)
            step(nc.vector.tensor_tensor(interp, b6, b4, ALU.subtract))
            dve.wait_ge(a_dve, 8)
            step(nc.vector.memset(b5[:, :], 0.0))
            dve.wait_ge(h0_loaded, 32)

            def norm_dve(first, act_at):
                step(nc.vector.tensor_reduce(st(0), h_all[:, :, :], AX.X, ALU.add))
                dve.wait_ge(a_dve, first)
                step(nc.vector.scalar_tensor_tensor(t3(b3), wide(0), -1.0 / D, h_all[:, :, :], ALU.mult, ALU.add))
                dve.wait_ge(a_act, act_at)
                step(nc.vector.tensor_reduce(st(3), t3(b4), AX.X, ALU.add))
                dve.wait_ge(a_dve, first + 2)
                step(nc.vector.tensor_scalar(st(1), st(3), 1.0 / D, EPS, ALU.mult, ALU.add))
                dve.wait_ge(a_act, act_at + 1)
                link(nc.vector.reciprocal(st(4), st(2)))

            norm_dve(10, 6)
            nc.vector.memset(stats[:, 7, :], 0.0).then_inc(h1_done, 1)
            xs = b6[:, 0:512].rearrange("p (t f) -> p t f", t=8)
            with dve.Fori(0, 8) as a:
                nc.vector.tensor_tensor(
                    xs, t3(b3)[:, bass.ds(a * 8, 8), :],
                    stats[:, 4, bass.ds(a * 8, 8)].unsqueeze(2).broadcast_to([128, 8, D]), ALU.mult).then_inc(xs_done, 1)
                dve.wait_ge(xw_pe, a + 1)
                nc.vector.tensor_copy(b4[0:D, 1024:2048].rearrange("p (c n) -> p c n", c=2), ybank[1][0:D])\
                    .then_inc(xw_dve, 1)
                for y in range(2):
                    dve.wait_ge(s_pe, 2 * a + y + 1)
                    nc.vector.tensor_reduce(
                        stats[:, 7, 4 * y:4 * y + 4],
                        ybank[y][:, :, :].rearrange("p c (t m) -> p (c t) m", t=2)[:, :, 0:NW],
                        AX.X, ALU.max, negate=True).then_inc(smax_link, 1)
                    dve.wait_ge(smax_link, 2 * a + y + 1)
                    nc.vector.tensor_scalar(stats[:, 5, 4 * y:4 * y + 4], stats[:, 7, 4 * y:4 * y + 4], 0.125, None,
                                            ALU.mult).then_inc(smax_done, 1)
                for i in range(2):
                    dve.wait_ge(pt_pe, 4 * a + i + 3)
                    nc.vector.tensor_copy(b2[:, 512 * (2 + i):512 * (3 + i)], bank[6 + i]).then_inc(pt_dve, 1)
                nc.vector.reciprocal(stats[:, 7, 8:16], stats[:, 6, 0:8]).then_inc(r_link, 1)
                dve.wait_ge(r_link, 2 * a + 1)
                dve.wait_ge(msg_pe, a + 1)
                nc.vector.tensor_tensor(b6[:, 1024:1536].rearrange("p (t f) -> p t f", t=8),
                                        ybank[0][:, 0, :].rearrange("p (t f) -> p t f", t=8),
                                        stats[:, 7, 8:16].unsqueeze(2).broadcast_to([128, 8, D]), ALU.mult)\
                    .then_inc(r_link, 1)
                dve.wait_ge(r_link, 2 * a + 2)
                hv = h_all[:, bass.ds(a * 8, 8), :]
                nc.vector.tensor_tensor(hv, hv, b6[:, 1024:1536].rearrange("p (t f) -> p t f", t=8), ALU.add)\
                    .then_inc(h1_done, 1)
            dve.wait_ge(h1_done, 9)
            norm_dve(14, 8)
            for g in range(4):
                c = slice(TILES // 4 * g, TILES // 4 * (g + 1))
                step(nc.vector.tensor_tensor(t3(b6)[:, c], t3(b3)[:, c], wide(4)[:, c], ALU.mult))
                dve.wait_ge(a_dve, 18 + 3 * g)
                step(nc.vector.tensor_scalar(z_parts[:, c, 0, :].bitcast(I32), t3(b6)[:, c].bitcast(I32), HIGH_BITS, None,
                                             ALU.bitwise_and))
                dve.wait_ge(a_dve, 19 + 3 * g)
                step(nc.vector.tensor_tensor(z_parts[:, c, 1, :], t3(b6)[:, c], z_parts[:, c, 0, :], ALU.subtract))

            def slot(it, s):
                starts, select, gather, attend, finish = flags(it)
                pair = pair_of(it, s)
                if pair:
                    n, u, own = pair
                    wait(dve, e_done, n + 1)
                    nc.vector.scalar_tensor_tensor(wgt[:, u % WBUF, :, :], ybank[s % 2][:, :, :], 0.0, wgt[:, u % WBUF, :, :],
                                                   ALU.is_ge, ALU.mult).then_inc(w_done, 1)
                prev = pair_of(it, s, LEAD - 1)
                if prev:
                    n, u, own = prev
                    if u in DVE_HIGH:
                        wait(dve, gather_done, n - WBUF + 1)
                        wait(dve, w_done, n + 1)
                        nc.vector.tensor_copy(w_high[:, u % WBUF, :, :], wgt[:, u % WBUF, :, :]).then_inc(high_dve, 1)
                late = pair_of(it, s, LBUF - 1)
                if late:
                    n, u, own = late
                    if u in DVE_LOW:
                        wait(dve, *made(own, u, DVE_HIGH, high_dve, high_act))
                        wait(dve, gather_done, n - LBUF + 1)
                        nc.vector.tensor_tensor(w_low[:, u % LBUF, :, :], wgt[:, u % WBUF, :, :],
                                                w_high[:, u % WBUF, :, :].bitcast(F32), ALU.subtract).then_inc(low_dve, 1)
                if s == 0 and attend:
                    j = it - 1
                    wait(dve, kva_act, j + 1)
                    wait(dve, gather_done, PAIRS * (j + 1))
                    wait(dve, kvn_pe, j)
                    nc.vector.tensor_tensor(kv_t, acc[1][:, :], kv_a, ALU.add).then_inc(kvt_dve, 1)
                if s == 2 and attend:
                    j = it - 1
                    wait(dve, kvn_pe, j + 1)
                    wait(dve, rz_link, j + 1)
                    wait(dve, o_pe, j)
                    nc.vector.tensor_tensor(kv_n[:, :, :], misc[0][:, :].rearrange("p (t d) -> p t d", t=GT),
                                            rz[:, :].unsqueeze(2).broadcast_to([128, GT, 128]), ALU.mult)\
                        .then_inc(kvn_dve, 1)
                if s == 3 and gather:
                    wait(dve, select_step, SEL * it + SEL)
                    wait(dve, rzn_done, it + 1)
                    wait(dve, kvn_dve, it)
                    nc.vector.tensor_copy(rz[:, :], rz_new[:, :]).then_inc(rz_link, 1)
                if s in (7, 8) and attend:
                    j, x = it - 1, s - 7
                    wait(dve, sim_pe, 2 * j + x + 1)
                    nc.vector.tensor_tensor(simm[:, x, :], misc[x][:, 0:384], causal[:, :], ALU.add)\
                        .then_inc(sim_link, 1)
                    wait(dve, sim_link, 2 * j + x + 1)
                    nc.vector.tensor_reduce(nmax[:, 2 * x:2 * x + 1], simm[:, x, 0:128], AX.X, ALU.max, negate=True)\
                        .then_inc(simm_dve, 1)
                    nc.vector.tensor_reduce(nmax[:, 2 * x + 1:2 * x + 2], simm[:, x, 128:384], AX.X, ALU.max,
                                            negate=True).then_inc(simm_dve, 1)
                if s == 0 and finish:
                    j = it - 2
                    wait(dve, prob_act, 2 * j + 2)
                    nc.vector.reciprocal(rl[:, :], lsum[:, :]).then_inc(rl_link, 1)
                if s == 1 and finish:
                    j = it - 2
                    wait(dve, rl_link, 2 * j + 1)
                    wait(dve, y_pe, j + 1)
                    nc.vector.tensor_tensor(y_n[:, :, :], misc[1][:, 0:256].rearrange("p (t f) -> p t f", t=GT),
                                            rl[:, :].unsqueeze(2).broadcast_to([128, GT, D]), ALU.mult)\
                        .then_inc(rl_link, 1)
                if s == 2 and finish:
                    j = it - 2
                    wait(dve, rl_link, 2 * j + 2)
                    if static(j):
                        hv = h_all[:, GT * (j % GROUPS):GT * (j % GROUPS) + GT, :]
                    else:
                        hv = h_all[:, bass.ds((j % GROUPS) * GT, GT), :]
                    nc.vector.tensor_tensor(hv, hv, y_n[:, :, :], ALU.add).then_inc(h_dve, 1)
                if starts if s > 10 else select:
                    part_of = it + 2 if s > 10 else it + 1
                    select_wait(part_of, s)
                    select_part(part_of, s)

            AFTER = {12: 1, 13: 2, 14: 3, 15: 4, 0: 5, 1: 6, 2: 7, 3: 8, 4: 11, 5: 12, 6: 13}

            def select_wait(j, s):
                if s == 11:
                    wait(dve, score_act, j + 1)
                if s in AFTER:
                    wait(dve, select_step, SEL * j + AFTER[s])
                if s in (0, 1, 2, 11, 12, 13, 15):
                    nc.vector.tensor_copy(gate[:, 0:1], gate[:, 1:2])
                if s == 5:
                    wait(dve, quad_pe, 4 * j)
                if s == 9:
                    wait(dve, wexp_act, j + 1)

            def select_part(j, s):
                def done(ins):
                    ins.then_inc(select_step, 1)

                halves = [(t, p) for t in range(GT) for p in range(2)]
                if s == 11:
                    for t, p in halves:
                        last = nc.vector.max(top[:, t, p, 0:8], score[:, t, p, :])
                    done(last)
                if s == 12:
                    for t, p in halves:
                        last = nc.vector.match_replace(score_m[:, t, p, :], top[:, t, p, 0:8], score[:, t, p, :], LOW)
                    done(last)
                if s == 13:
                    for t, p in halves:
                        last = nc.vector.max(top[:, t, p, 8:16], score_m[:, t, p, :])
                    done(last)
                if s == 14:
                    at = 0
                    for lo, hi, n in CAND:
                        m = hi - lo
                        last = nc.vector.tensor_tensor(
                            cand[:, :, at:at + m * n].rearrange("p t (i k) -> p t i k", i=m),
                            top[:, :, 0, lo:hi].unsqueeze(3).broadcast_to([128, GT, m, n]),
                            top[:, :, 1, 0:n].unsqueeze(2).broadcast_to([128, GT, m, n]), ALU.add)
                        at += m * n
                    done(last)
                if s in (15, 1):
                    source, at = ((cand, 0), (cand_m, 8))[s == 1]
                    for t in range(GT):
                        last = nc.vector.max(best[:, t, at:at + 8], source[:, t, :])
                    done(last)
                if s in (0, 2):
                    source, left, at = ((cand, cand_m, 0), (cand_m, cand_mm, 8))[s // 2]
                    for t in range(GT):
                        last = nc.vector.match_replace(left[:, t, :], best[:, t, at:at + 8], source[:, t, :], LOW)
                    done(last)
                if s == 3:
                    nc.vector.tensor_scalar(small[:, 2, :], best[:, :, 0], -SPREAD, None, ALU.add)
                    done(nc.vector.tensor_reduce(small[:, 0, :], cand_mm[:, :, :], AX.X, ALU.max))
                    wait(dve, select_step, SEL * j + 9)
                    done(nc.vector.tensor_tensor(small[:, 1, :], small[:, 0, :], best[:, :, 15], ALU.add))
                    wait(dve, select_step, SEL * j + 10)
                    done(nc.vector.scalar_tensor_tensor(small[:, 3, :], small[:, 1, :], 0.5, small[:, 2, :],
                                                        ALU.mult, ALU.max))
                if s == 4:
                    thr = small[:, 3, :].unsqueeze(2)
                    nc.vector.tensor_tensor(wsel[:, :, :], best[:, :, :], thr.broadcast_to([128, GT, TOPK]), ALU.subtract)
                    done(nc.vector.tensor_tensor(shifted[:, :, :], score[:, :, 1, :],
                                                 thr.broadcast_to([128, GT, NK]), ALU.subtract))
                if s == 5:
                    for high, _low, src in PLACES:
                        last = nc.vector.tensor_scalar(high.bitcast(I32), src.bitcast(I32), HIGH_BITS, None,
                                                       ALU.bitwise_and)
                    done(last)
                if s == 6:
                    for high, low, src in PLACES:
                        last = nc.vector.tensor_tensor(low, src, high, ALU.subtract)
                    done(last)
                if s == 9:
                    nc.vector.scalar_tensor_tensor(wbest[:, :, :], wsel[:, :, :], 0.0, wbest[:, :, :],
                                                   ALU.is_ge, ALU.mult).then_inc(rzn_link, 1)
                    wait(dve, rzn_link, 2 * j + 1)
                    nc.vector.tensor_reduce(small[:, 4, :], wbest[:, :, :], AX.X, ALU.add).then_inc(rzn_link, 1)
                    wait(dve, rzn_link, 2 * j + 2)
                    nc.vector.reciprocal(rz_new[:, :], small[:, 4, :]).then_inc(rzn_done, 1)

            def body(it):
                for s in range(PAIRS):
                    slot(it, s)

            run_iterations(dve, body)


def interpolation_weights():
    import numpy as np
    f = np.float32
    n = L
    count = int((n - 1) / 0.25) + 1
    step = np.arange(count - 1, dtype=f) * (f(1) / f(count - 1))
    x = np.concatenate([step, np.ones(1, f)]) * f(n - 1)
    x = np.concatenate([x, np.full(L * UP - count, x[-1], f)])
    i0 = np.floor(x).astype(np.int32)
    frac = x - i0.astype(f)
    a = f(-0.75)
    out = np.zeros((TAPS, L * UP), f)
    p = np.arange(L * UP)
    for off in range(-1, 3):
        at = np.abs(frac - f(off))
        near = ((a + f(2)) * at - (a + f(3))) * at * at + f(1)
        far = ((a * at - f(5) * a) * at + f(8) * a) * at - f(4) * a
        w = np.where(at <= 1, near, np.where(at < 2, far, f(0)))
        k = i0 + off - p // UP + 2
        ok = (k >= 0) & (k < TAPS)
        out[k[ok], p[ok]] += w[ok]
    return np.ascontiguousarray(out.reshape(TAPS, QUARTERS, PTS).transpose(1, 0, 2))


def dft_matrix():
    import numpy as np
    n = np.arange(WIN)
    ang = 2 * np.pi * (n[:, None] * n[None, :] % WIN) / WIN
    m = np.concatenate([np.cos(ang), np.sin(ang)], 1).astype(np.float32)
    return np.concatenate([m, m], 0)


def onehot_matrices():
    import numpy as np
    m = np.zeros((128, 2, 8, 128), np.float32)
    for swap in range(2):
        for r in range(8):
            for jj in range(4):
                for ii in range(32):
                    for part in (0, 32):
                        m[64 * swap + part + ii, swap, r, 32 * jj + ii] = 1
                        m[64 * (1 - swap) + part + 4 * r + jj, swap, r, 32 * jj + ii] = 1
    return m


def causal_mask():
    import numpy as np
    tri = np.where(np.arange(128)[:, None] >= np.arange(128)[None, :], 0, LOW).astype(np.float32)
    return np.concatenate([tri, np.zeros((128, 128), np.float32), tri], 1)


def kernel(x, L0_attn_W, L0_ffn_Wq_pk, L0_ffn_pk_keys, L0_ffn_Wq, L0_ffn_keys_table, L0_ffn_values_table, L0_ffn_Wo):
    import numpy as np
    import concourse.bacc as bacc
    from concourse.bass_utils import run_bass_kernel_spmd

    x = np.asarray(x)
    xp = np.concatenate([x[:, :1], x[:, :1], x, x[:, -1:], x[:, -1:]], 1)
    wqpk = np.asarray(L0_ffn_Wq_pk).reshape(D, 2, HEADS, 32).transpose(3, 2, 1, 0).reshape(32, 2 * HEADS, D)
    keys = np.asarray(L0_ffn_pk_keys).transpose(3, 2, 0, 1).reshape(32, 2 * HEADS, NK)
    kv = np.concatenate([np.asarray(L0_ffn_keys_table), np.asarray(L0_ffn_values_table)], 1)
    kv = kv.reshape(HEADS, 2, 8, 4, 2, 32, 2 * D).transpose(0, 3, 5, 4, 1, 2, 6).reshape(HEADS, 128, 2, 2, 8, 2 * D)
    kv = np.concatenate([kv[:, :, ka, kb] for ka, kb in QUADS], 2)
    arrays = {
        "xp": xp, "interp_w": interpolation_weights(), "dft": dft_matrix(), "ident": np.eye(128, dtype=np.float32),
        "onehot": onehot_matrices(), "causal": causal_mask(), "attn_w": np.asarray(L0_attn_W), "wqpk_t": wqpk,
        "keys_t": keys, "table": kv, "wq_d": np.asarray(L0_ffn_Wq).reshape(D, HEADS, D),
        "wo_d": np.asarray(L0_ffn_Wo).reshape(HEADS, D, D),
    }
    arrays = {"in_" + n: np.ascontiguousarray(a) for n, a in arrays.items()}
    nc = bacc.Bacc("TRN2", target_bir_lowering=False, num_devices=1)
    args = [nc.dram_tensor(n, a.shape, mybir.dt.from_np(a.dtype), kind="ExternalInput").ap() for n, a in arrays.items()]
    args.append(nc.dram_tensor("out", (B, NW, D), F32, kind="ExternalOutput").ap())
    program(nc, *args)
    r = run_bass_kernel_spmd(nc, [arrays], core_ids=[0])
    return r.results[0]["out"]
```
